# Optimizing a Trainium2 kernel written in Bass

```python
import numpy as np
import jax
import jax.numpy as jnp

def _softmax(x, axis=-1):
    return jax.nn.softmax(x, axis=axis)

def _gelu(x):
    return jax.nn.gelu(x, approximate=True)

def _silu(x):
    return jax.nn.silu(x)

def _sigmoid(x):
    return jax.nn.sigmoid(x)

def _layernorm(x, axis=-1, eps=1e-05):
    m = jnp.mean(x, axis=axis, keepdims=True)
    v = jnp.var(x, axis=axis, keepdims=True)
    return (x - m) / jnp.sqrt(v + eps)

def _scatter_add(tgt, idx, src, axis=0):
    return tgt.at[idx].add(src)

def _segment_sum(src, seg, n):
    return jax.ops.segment_sum(src, seg, n)
kernel_name = 'mk_recurrent_d1_jaxref_r4_f56dfe'

def setup_inputs(seed: int=0):
    np.random.seed(seed)
    _w = jnp.asarray

    def _L0_attn_setup():
        import jax, jax.numpy as jnp
        import numpy as np
        HEADS = 16
        key = jax.random.key(seed)
        ks = jax.random.split(key, 5)
        B, T, D = (2, 512, 512)
        s = 0.02
        return {'x': jax.random.normal(ks[0], (B, T, D), dtype=jnp.float32), 'Wq': jax.random.normal(ks[1], (D, D), dtype=jnp.float32) * s, 'Wk': jax.random.normal(ks[2], (D, D), dtype=jnp.float32) * s, 'Wv': jax.random.normal(ks[3], (D, D), dtype=jnp.float32) * s, 'Wo': jax.random.normal(ks[4], (D, D), dtype=jnp.float32) * s}
    _L0_attn_in = _L0_attn_setup()

    def _L0_ffn_setup():
        import jax, jax.numpy as jnp
        import numpy as np
        LN_EPS = 1e-05
        Q_EPS = 1e-05

        def ternary_quantize(w):
            scale = jnp.mean(jnp.abs(w))
            return jnp.clip(jnp.round(w / (scale + Q_EPS)), -1.0, 1.0)

        def layernorm(x, gamma, beta):
            mu = jnp.mean(x, axis=-1, keepdims=True)
            var = jnp.mean(jnp.square(x - mu), axis=-1, keepdims=True)
            return (x - mu) * jax.lax.rsqrt(var + LN_EPS) * gamma + beta
        key = jax.random.key(seed)
        k_x, k_w = jax.random.split(key)
        B, S, D_IN, D_OUT = (4, 512, 512, 512)
        x = jax.random.normal(k_x, (B, S, D_IN), dtype=jnp.float32)
        std = np.sqrt(2.0 / D_OUT).astype(np.float32)
        weight = jax.random.normal(k_w, (D_OUT, D_IN), dtype=jnp.float32) * std
        bias = jnp.zeros((D_OUT,), dtype=jnp.float32)
        ln_gamma = jnp.ones((D_IN,), dtype=jnp.float32)
        ln_beta = jnp.zeros((D_IN,), dtype=jnp.float32)
        return {'x': x, 'weight': weight, 'bias': bias, 'ln_gamma': ln_gamma, 'ln_beta': ln_beta}
    _L0_ffn_in = _L0_ffn_setup()
    _d = {'L0_attn_x': _L0_attn_in['x'], 'L0_attn_Wq': _L0_attn_in['Wq'], 'L0_attn_Wk': _L0_attn_in['Wk'], 'L0_attn_Wv': _L0_attn_in['Wv'], 'L0_attn_Wo': _L0_attn_in['Wo'], 'L0_ffn_weight': _L0_ffn_in['weight'], 'L0_ffn_bias': _L0_ffn_in['bias'], 'L0_ffn_ln_gamma': _L0_ffn_in['ln_gamma'], 'L0_ffn_ln_beta': _L0_ffn_in['ln_beta']}
    _x0 = _d['L0_attn_x']
    _d['L0_attn_x'] = jax.random.normal(jax.random.fold_in(jax.random.key(seed), 1), (2, 2048, 512), dtype=_x0.dtype)
    del _x0
    return _d

def reference(L0_attn_x, L0_attn_Wq, L0_attn_Wk, L0_attn_Wv, L0_attn_Wo, L0_ffn_weight, L0_ffn_bias, L0_ffn_ln_gamma, L0_ffn_ln_beta):

    def _L0_attn_ref(x, Wq, Wk, Wv, Wo):
        import jax, jax.numpy as jnp
        import numpy as np
        HEADS = 16
        B, T, _ = x.shape
        H = HEADS
        Dh = Wq.shape[1] // H
        q = (x @ Wq).reshape(B, T, H, Dh)
        k = (x @ Wk).reshape(B, T, H, Dh)
        v = (x @ Wv).reshape(B, T, H, Dh)
        scores = jnp.einsum('bthd,bshd->bhts', q, k)
        mask = jnp.tril(jnp.ones((T, T), dtype=scores.dtype))
        scores = scores * mask
        attn = jax.nn.softmax(scores / T ** 0.5, axis=-1)
        out = jnp.einsum('bhts,bshd->bthd', attn, v).reshape(B, T, H * Dh)
        return out @ Wo

    def _L0_ffn_ref(x, weight, bias, ln_gamma, ln_beta):
        import jax, jax.numpy as jnp
        import numpy as np
        LN_EPS = 1e-05
        Q_EPS = 1e-05

        def ternary_quantize(w):
            scale = jnp.mean(jnp.abs(w))
            return jnp.clip(jnp.round(w / (scale + Q_EPS)), -1.0, 1.0)

        def layernorm(x, gamma, beta):
            mu = jnp.mean(x, axis=-1, keepdims=True)
            var = jnp.mean(jnp.square(x - mu), axis=-1, keepdims=True)
            return (x - mu) * jax.lax.rsqrt(var + LN_EPS) * gamma + beta
        xn = layernorm(x, ln_gamma, ln_beta)
        w_q = ternary_quantize(weight)
        return jnp.einsum('bsi,oi->bso', xn, w_q) + bias
    x = L0_attn_x
    xn = _layernorm(x, axis=-1)
    s = _L0_attn_ref(xn, L0_attn_Wq, L0_attn_Wk, L0_attn_Wv, L0_attn_Wo)
    g = _silu(_L0_ffn_ref(xn, L0_ffn_weight, L0_ffn_bias, L0_ffn_ln_gamma, L0_ffn_ln_beta))
    x = x + s * g
    return x

_drawn_inputs = setup_inputs


def setup_inputs(seed=0):
    import zlib

    import numpy as np

    out = dict(_drawn_inputs(seed))
    spreads = {'L0_ffn_bias': (0.0, 0.8), 'L0_ffn_ln_gamma': (1.0, 0.6), 'L0_ffn_ln_beta': (0.0, 0.8)}
    factors = {'L0_attn_Wq': 8.0, 'L0_attn_Wk': 8.0}
    for name, (base, spread) in spreads.items():
        noise = np.random.default_rng([zlib.crc32(name.encode()), seed]).standard_normal(out[name].shape)
        drawn = base * np.exp(spread * noise) if base else spread * noise
        out[name] = jnp.asarray(drawn.astype(out[name].dtype))
    for name, factor in factors.items():
        out[name] = (out[name] * factor).astype(out[name].dtype)
    return out
```

```python
from contextlib import ExitStack

import concourse.bass as bass
from concourse import mybir

F32 = mybir.dt.float32
F32R = mybir.dt.float32r
BF16 = mybir.dt.bfloat16
F16 = mybir.dt.float16
ACT = mybir.ActivationFunctionType
ALU = mybir.AluOpType
AX = mybir.AxisListType

P = 128
B, T, D, H = 2, 2048, 512, 16
DH = D // H
KT = D // P
HQ = P // DH
NQ = H // HQ
NQUAD = B * NQ
CW = 512
NCH = T // CW
CT = CW // P
NT = T // P
SCALE = float(T) ** -0.5
EPS = 1e-5
BIG = 1e30
STACK = 3 * DH
MROW = STACK
M0ROW = STACK + 1
NSTEP = sum(CT * c + CT for c in range(NCH))
STEPS = [(c, j) for c in range(NCH) for j in range(CT * c + CT)]
NPAIR = HQ // 2
ONE = 1


def max_banks():
    banks = []
    for i in range(NT):
        for f in range((i + 1) // CT):
            banks.append(([(i, f * CW, CW)], i * CT + f, 1))
    for r in range(1, CT):
        w = r * P
        per = CW // w
        tiles = [i for i in range(NT) if (i + 1) % CT == r]
        for a in range(0, len(tiles), per):
            part = tiles[a:a + per]
            slots = [i * CT + (i + 1) // CT for i in part]
            banks.append(([(i, (i + 1) // CT * CW, w) for i in part], slots[0], CT * CT + 1))
    return banks


MAXB = max_banks()
NMB = HQ * len(MAXB)


def build(nc, x, Wq, Wk, Wv, Wo, Wf, bias, gamma, beta, out):
    top = ExitStack()
    with top:
        def sem(name):
            return top.enter_context(nc.semaphore(name))

        def sbuf(stack, name, shape, dt):
            return stack.enter_context(nc.sbuf_tensor(name, shape, dt))

        def psum(stack, name, shape):
            return stack.enter_context(nc.psum_tensor(name, shape, F32))

        q_hi = nc.dram_tensor("q_hi", [B * D, T], F32).ap()
        q_lo = nc.dram_tensor("q_lo", [B * D, T], F32).ap()
        k_hi = nc.dram_tensor("k_hi", [B * D, T], F32).ap()
        k_lo = nc.dram_tensor("k_lo", [B * D, T], F32).ap()
        v_quad = nc.dram_tensor("v_quad", [NQUAD * P, NT * P], F32).ap()
        v_cum = nc.dram_tensor("v_cum", [B * D, T], F32).ap()
        gate = nc.dram_tensor("gate", [B * T, D], F32).ap()
        att_t = nc.dram_tensor("att_t", [B * D, T], F32).ap()

        ident = sbuf(top, "ident", [P, P], F32)
        ones = sbuf(top, "ones", [P, P], F32)

        pa = ExitStack()
        w_hi = [sbuf(pa, f"w_hi{i}", [P, KT, D], F32R) for i in range(3)]
        w_lo = [sbuf(pa, f"w_lo{i}", [P, KT, D], F32R) for i in range(3)]
        wf_t = sbuf(pa, "wf_t", [P, KT, D], F32R)
        xt = [sbuf(pa, f"xt{i}", [P, CT, D], F32) for i in range(2)]
        xn = sbuf(pa, "xn", [P, CT, D], F32)
        zn = sbuf(pa, "zn", [P, CT, D], F32)
        xh = sbuf(pa, "xh", [P, KT, CW], F32R)
        xl = sbuf(pa, "xl", [P, KT, CW], F32R)
        yf = [sbuf(pa, f"yf{i}", [P, CW], F32) for i in range(2)]
        yh = sbuf(pa, "yh", [P, KT, CW], F32R)
        yl = sbuf(pa, "yl", [P, KT, CW], F32R)
        st_hi = [sbuf(pa, f"st_hi{i}", [P, CW], F32R) for i in range(4)]
        st_lo = [sbuf(pa, f"st_lo{i}", [P, CW], F32R) for i in range(4)]
        vs = sbuf(pa, "vs", [P, CT, D], F32)
        cs = [sbuf(pa, f"cs{i}", [P, CW], F32) for i in range(NQ)]
        carry = sbuf(pa, "carry", [P, NQ], F32)
        zb = [sbuf(pa, f"zb{i}", [P, D], F32) for i in range(2)]
        gs = [sbuf(pa, f"gs{i}", [P, D], F32) for i in range(2)]
        bias_b = sbuf(pa, "bias_b", [P, D], F32)
        zeros = sbuf(pa, "zeros", [P, CW], F32)
        gam = sbuf(pa, "gam", [P, KT], F32)
        bet = sbuf(pa, "bet", [P, KT], F32)
        stats = sbuf(pa, "stats", [P, CT, 6], F32)
        mv = [sbuf(pa, f"mv{i}", [P, CT, 2], F32) for i in range(2)]
        ve = [sbuf(pa, f"ve{i}", [P, CT], F32) for i in range(2)]
        rstd = [sbuf(pa, f"rstd{i}", [P, CT], F32) for i in range(2)]
        mhalf = sbuf(pa, "mhalf", [P, CT], F32)
        wabs = sbuf(pa, "wabs", [P, 1], F32)
        wsc = sbuf(pa, "wsc", [P, 4], F32)
        psT = [psum(pa, f"psT{i}", [P, CW]) for i in range(2)]
        psP = [psum(pa, f"psP{i}", [P, CW]) for i in range(4)]
        psW = psum(pa, "psW", [P, CW])
        pa.close()

        pc = ExitStack()
        Qs = [sbuf(pc, f"Qs{i}", [P, HQ, T], F32R) for i in range(2)]
        Ks = [sbuf(pc, f"Ks{i}", [P, HQ, T], F32R) for i in range(2)]
        Vs = [sbuf(pc, f"Vs{i}", [P, NT, P], F32) for i in range(2)]
        Pb = [[sbuf(pc, f"Pb{i}_{p}", [P, 2, CW], F32) for p in range(NPAIR)] for i in range(2)]
        acc = [[sbuf(pc, f"acc{i}_{p}", [P, 2, CW], F32) for p in range(NPAIR)] for i in range(2)]
        cum = sbuf(pc, "cum", [P, T], F32)
        later = sbuf(pc, "later", [P, T], F16)
        Eb = sbuf(pc, "Eb", [P, CW], F32)
        SE = sbuf(pc, "SE", [P, CW], F32)
        NE = sbuf(pc, "NE", [P, CW], F32)
        num = sbuf(pc, "num", [P, CW], F32)
        ost = [sbuf(pc, f"ost{i}", [P, CW], F32) for i in range(2)]
        esel = sbuf(pc, "esel", [P, HQ, P], F32R)
        identb = sbuf(pc, "identb", [P, P], BF16)
        negm = sbuf(pc, "negm", [P, P], BF16)
        zrow = sbuf(pc, "zrow", [P, HQ, NT], F32)
        mx = sbuf(pc, "mx", [P, HQ * NT, CT], F32)
        mred = sbuf(pc, "mred", [P, HQ * NT], F32)
        mmax = sbuf(pc, "mmax", [P, HQ * NT], F32)
        mneg = sbuf(pc, "mneg", [P, 2 * HQ * NT], F32R)
        mrow = sbuf(pc, "mrow", [P, P], F32R)
        psS = [psum(pc, f"psS{i}", [P, 2, CW]) for i in range(2)]
        psM = [psum(pc, f"psM{i}", [P, CW]) for i in range(2)]
        psO = psum(pc, "psO", [P, CW])
        psL = psum(pc, "psL", [P, CW])
        pc.close()

        pd = ExitStack()
        wo = sbuf(pd, "wo", [P, KT, D], F32)
        ac = [sbuf(pd, f"ac{i}", [P, KT, CW], F32) for i in range(2)]
        xr = [sbuf(pd, f"xr{i}", [P, CT, D], F32) for i in range(2)]
        gr = [sbuf(pd, f"gr{i}", [P, CT, D], F32) for i in range(2)]
        oo = [sbuf(pd, f"oo{i}", [P, CT, D], F32) for i in range(2)]
        sg = [sbuf(pd, f"sg{i}", [P, D], F32) for i in range(2)]
        psD = [psum(pd, f"psD{i}", [P, D]) for i in range(8)]
        pd.close()

        const_a = sem("const_a")
        bias_in = sem("bias_in")
        xt_in = [sem(f"xt_in{i}") for i in range(2)]
        xt_used = sem("xt_used")
        wabs_done = sem("wabs_done")
        wtot_done = sem("wtot_done")
        wprep = sem("wprep")
        tern_done = sem("tern_done")
        wf_done = sem("wf_done")
        T_full = sem("T_full")
        P_full = sem("P_full")
        ln_own = sem("ln_own")
        dve_waited = sem("dve_waited")
        ve_done = sem("ve_done")
        rstd_done = sem("rstd_done")
        zn_done = sem("zn_done")
        xh_done = sem("xh_done")
        xl_done = sem("xl_done")
        yf_done = sem("yf_done")
        yh_done = sem("yh_done")
        yl_done = sem("yl_done")
        hi_done = sem("hi_done")
        lo_done = sem("lo_done")
        st_out = [sem(f"st_out{i}") for i in range(4)]
        vs_done = sem("vs_done")
        vs_out = sem("vs_out")
        cs_done = sem("cs_done")
        carry_done = sem("carry_done")
        cs_out = [sem(f"cs_out{i}") for i in range(NQ)]
        zb_done = sem("zb_done")
        gs_done = sem("gs_done")
        gs_out = [sem(f"gs_out{i}") for i in range(2)]
        const_c = sem("const_c")
        kq_in = [sem(f"kq_in{i}") for i in range(2)]
        v_in = [sem(f"v_in{i}") for i in range(2)]
        cum_in = sem("cum_in")
        M_full = sem("M_full")
        mx_done = sem("mx_done")
        mred_done = sem("mred_done")
        mneg_done = sem("mneg_done")
        L_full = sem("L_full")
        mrow_done = sem("mrow_done")
        mrow_in = sem("mrow_in")
        S_full = sem("S_full")
        exp_done = sem("exp_done")
        pool_waited = sem("pool_waited")
        mask_done = sem("mask_done")
        pv_done = sem("pv_done")
        sum_done = sem("sum_done")
        E_done = sem("E_done")
        sub_done = sem("sub_done")
        SE_done = sem("SE_done")
        NE_done = sem("NE_done")
        num_done = sem("num_done")
        add_done = sem("add_done")
        den_done = sem("den_done")
        ost_done = sem("ost_done")
        ost_out = [sem(f"ost_out{i}") for i in range(2)]
        wo_in = sem("wo_in")
        d_in = [sem(f"d_in{i}") for i in range(2)]
        D_full = sem("D_full")
        sg_done = sem("sg_done")
        oo_done = sem("oo_done")
        oo_out = [sem(f"oo_out{i}") for i in range(2)]

        x_v = x.rearrange("b (c j p) d -> (b c) p j d", p=P, j=CT)
        out_v = out.rearrange("b (c j p) d -> (b c) p j d", p=P, j=CT)
        gate_t = gate.rearrange("(n p) d -> n p d", p=P)
        gate_v = gate.rearrange("(n j p) d -> n p j d", p=P, j=CT)
        w_q, w_k, w_v, w_o, w_f = (w.rearrange("(k p) n -> p k n", p=P) for w in (Wq, Wk, Wv, Wo, Wf))
        NTU = 3 * KT
        NPU = 3 * KT + CT
        NLU = 1 + 2 * NCH
        NCHUNK = B * NCH
        last_step = [STEPS.index((c, CT * c + CT - 1)) for c in range(NCH)]

        credited = [P_full, yl_done, vs_out, gs_done, cs_done, zb_done, carry_done, num_done, ost_done, add_done, L_full, mrow_in, pv_done, sum_done, NE_done, exp_done, mx_done, sub_done, oo_done, sg_done, E_done,
                    *st_out, *gs_out, *cs_out, *ost_out, *oo_out]

        block = top.enter_context(nc.Block())

        def phase_a_over(eng):
            for s in range(4):
                eng.wait_ge(st_out[s], ONE + NCHUNK * 2 * 32)
            eng.wait_ge(vs_out, ONE + NCHUNK * NQ * 16)
            for m in range(NQ):
                eng.wait_ge(cs_out[m], ONE + NCHUNK * 16)
            for s in range(2):
                eng.wait_ge(gs_out[s], ONE + NCHUNK * (CT // 2) * 16)
            eng.wait_ge(carry_done, ONE + NCHUNK * NQ)
            eng.wait_ge(T_full, KT + NCHUNK * NTU)
            eng.wait_ge(P_full, ONE + NCHUNK * NPU)

        def attention_over(eng):
            for s in range(2):
                eng.wait_ge(ost_out[s], ONE + NQUAD * NCH // 2 * 16)
            eng.wait_ge(L_full, ONE + NQUAD * NLU)
            eng.wait_ge(kq_in[0], (NQUAD // 2 + 1) * 96)
            eng.wait_ge(v_in[0], (NQUAD // 2 + 1) * 16)
            eng.wait_ge(NE_done, ONE + NQUAD * NCH)

        @block.sync
        def _(sp):
            sp.dma_start(xt[0][:], w_f).then_inc(xt_in[0], 16)
            sp.dma_start(xt[1][:], w_q).then_inc(xt_in[1], 16)
            for s in credited:
                sp.sem_inc(s, ONE)
            for k in range(KT):
                sp.dma_start(gam[:, k:k + 1], gamma.rearrange("(k p u) -> k p u", p=P, u=1)[k]).then_inc(bias_in, 16)
                sp.dma_start(bet[:, k:k + 1], beta.rearrange("(k p u) -> k p u", p=P, u=1)[k]).then_inc(bias_in, 16)
            sp.dma_start(bias_b[:], bias.rearrange("(u n) -> u n", u=1).broadcast_to([P, D])).then_inc(bias_in, 16)
            sp.wait_ge(xt_used, 1)
            sp.dma_start(xt[0][:], w_k).then_inc(xt_in[0], 16)
            sp.wait_ge(xt_used, 2)
            sp.dma_start(xt[1][:], w_v).then_inc(xt_in[1], 16)

            with sp.Fori(0, B) as b:
                for c in range(NCH):
                    n = b * NCH + c
                    if c == 0:
                        sp.wait_ge(xt_used, n + 3)
                        sp.dma_start(xt[0][:], x_v[n]).then_inc(xt_in[0], 16)
                    if c < NCH - 1:
                        sp.wait_ge(xt_used, n + 4)
                        sp.dma_start(xt[(c + 1) % 2][:], x_v[n + 1]).then_inc(xt_in[(c + 1) % 2], 16)
                    cols = slice(c * CW, (c + 1) * CW)
                    for k in range(2 * NQ):
                        hi, lo = (q_hi, q_lo) if k < NQ else (k_hi, k_lo)
                        rows = bass.ds(b * D + (k % NQ) * P, P)
                        sp.wait_ge(hi_done, n * 2 * NQ + k + 1)
                        sp.dma_start(hi[rows, cols], st_hi[k % 4][:].bitcast(F32)).then_inc(st_out[k % 4], 16)
                        sp.wait_ge(lo_done, n * 2 * NQ + k + 1)
                        sp.dma_start(lo[rows, cols], st_lo[k % 4][:].bitcast(F32)).then_inc(st_out[k % 4], 16)
                    sp.wait_ge(vs_done, (n + 1) * CT)
                    for m in range(NQ):
                        sp.dma_start(v_quad[bass.ds(b * D + m * P, P), cols].rearrange("p (j n) -> p j n", n=P),
                                     vs[:, :, m * P:(m + 1) * P]).then_inc(vs_out, 16)
                    for j in range(CT):
                        sp.wait_ge(gs_done, ONE + n * CT + j + 1)
                        sp.dma_start(gate_t[n * CT + j], gs[j % 2][:]).then_inc(gs_out[j % 2], 16)
                    for m in range(NQ):
                        sp.wait_ge(cs_done, ONE + n * NQ + m + 1)
                        sp.dma_start(v_cum[bass.ds(b * D + m * P, P), cols], cs[m][:]).then_inc(cs_out[m], 16)

            phase_a_over(sp)

            def load_quad(qn, par):
                def heads(a):
                    return a[bass.ds(qn * P, P), :].rearrange("(h d) t -> d h t", d=DH)
                for g, (qa, ka) in enumerate(((q_hi, k_hi), (q_lo, k_hi), (q_hi, k_lo))):
                    rows = slice(g * DH, (g + 1) * DH)
                    sp.dma_start(Qs[par][rows, :, :].bitcast(F32), heads(qa)).then_inc(kq_in[par], 16)
                    sp.dma_start(Ks[par][rows, :, :].bitcast(F32), heads(ka)).then_inc(kq_in[par], 16)
                sp.dma_start(Vs[par][:], v_quad[bass.ds(qn * P, P), :].rearrange("p (j n) -> p j n", n=P)).then_inc(v_in[par], 16)

            load_quad(0, 0)
            with sp.Fori(0, NQUAD // 2) as i:
                for par in range(2):
                    qn = 2 * i + par
                    sp.wait_ge(sub_done, ONE + qn * NCH)
                    sp.dma_start(cum[:], v_cum[bass.ds(qn * P, P), :]).then_inc(cum_in, 16)
                    sp.wait_ge(L_full, ONE + qn * NLU)
                    load_quad(qn + 1 if par == 0 else (qn + 1) % NQUAD, 1 - par)
                    sp.wait_ge(mrow_done, qn + 1)
                    for r in range(2):
                        sp.dma_start(Qs[par][MROW + r:MROW + r + 1, :, :].bitcast(F32), mrow[r * HQ * NT:(r + 1) * HQ * NT, :].bitcast(F32)).then_inc(mrow_in, 16)
                    for c in range(NCH):
                        sp.wait_ge(ost_done, ONE + qn * NCH + c + 1)
                        sp.dma_start(att_t[bass.ds(qn * P, P), c * CW:(c + 1) * CW], ost[c % 2][:]).then_inc(ost_out[c % 2], 16)

            attention_over(sp)
            sp.dma_start(wo[:], w_o).then_inc(wo_in, 16)

            with sp.Fori(0, B) as b:
                for c in range(NCH):
                    n = b * NCH + c
                    if c == 0:
                        loads = (0, 1)
                    elif c < NCH - 1:
                        loads = (c + 1,)
                    else:
                        loads = ()
                    for l in loads:
                        m = b * NCH + l
                        sp.wait_ge(oo_done, ONE + ((b * NCH if l < 2 else m - 1) * CT))
                        rows = bass.ds(b * D, D)
                        sp.dma_start(ac[l % 2][:], att_t[rows, l * CW:(l + 1) * CW].rearrange("(k p) w -> p k w", p=P)).then_inc(d_in[l % 2], 16)
                        sp.dma_start(xr[l % 2][:], x_v[m]).then_inc(d_in[l % 2], 16)
                        sp.dma_start(gr[l % 2][:], gate_v[m]).then_inc(d_in[l % 2], 16)
                    sp.wait_ge(oo_done, ONE + (n + 1) * CT)
                    sp.dma_start(out_v[n], oo[c % 2][:]).then_inc(oo_out[c % 2], 16)
            for s in range(2):
                sp.wait_ge(oo_out[s], ONE + NCHUNK // 2 * 16)

        @block.gpsimd
        def _(pool):
            g = nc.gpsimd
            g.memset(ones[:], 1.0).then_inc(const_a, 1)
            g.memset(zeros[:], 0.0).then_inc(const_a, 1)
            g.memset(mhalf[:], -0.5).then_inc(const_a, 1)
            pool.wait_ge(const_a, 3)
            g.affine_select(out=ident[:], in_=ones[:], compare_op=ALU.is_equal, fill=0.0, base=0,
                            pattern=[[1, P]], channel_multiplier=-1).then_inc(const_a, 1)
            pool.wait_ge(const_a, 4)
            with pool.Fori(0, B) as b:
                for c in range(NCH):
                    n = b * NCH + c
                    for i in range(2):
                        pool.wait_ge(ve_done, 2 * n + i + 1)
                        g.tensor_tensor(rstd[i][:], ve[i][:], mhalf[:], ALU.pow).then_inc(rstd_done, 1)

            phase_a_over(pool)
            g.memset(Ks[0][MROW:MROW + 1, :, :].bitcast(F32), 1.0).then_inc(const_c, 1)
            pool.wait_ge(const_c, 1)
            g.memset(Ks[1][MROW:MROW + 1, :, :].bitcast(F32), 1.0).then_inc(const_c, 1)
            pool.wait_ge(const_c, 2)
            g.iota(later[:], pattern=[[-1, T]], base=T - 1, channel_multiplier=0,
                   allow_small_or_imprecise_dtypes=True).then_inc(const_c, 1)
            pool.wait_ge(const_c, 3)
            g.memset(mx[:], 0.0).then_inc(const_c, 1)
            pool.wait_ge(const_c, 4)
            g.tensor_copy(identb[:], ident[:]).then_inc(const_c, 1)
            pool.wait_ge(const_c, 5)
            g.memset(zrow[:], 0.0).then_inc(const_c, 1)
            pool.wait_ge(const_c, 6)
            g.affine_select(out=zrow[:], in_=zrow[:], compare_op=ALU.is_gt, fill=-BIG, base=P - 1,
                            pattern=[[0, HQ], [0, NT]], channel_multiplier=-1).then_inc(const_c, 1)
            pool.wait_ge(const_c, 7)
            g.memset(zrow[:, :, 0:NT - 1], 0.0).then_inc(const_c, 1)
            pool.wait_ge(const_c, 8)
            g.memset(negm[:], 0.0).then_inc(const_c, 1)
            pool.wait_ge(const_c, 9)
            g.affine_select(out=negm[:], in_=negm[:], compare_op=ALU.is_ge, fill=-BIG, base=0,
                            pattern=[[-1, P]], channel_multiplier=1).then_inc(const_c, 1)
            pool.wait_ge(const_c, 10)
            g.memset(esel[:].bitcast(F32), 0.0).then_inc(const_c, 1)
            pool.wait_ge(const_c, 11)
            for h in range(HQ):
                g.memset(esel[MROW:P, h, h * DH:(h + 1) * DH].bitcast(F32), 1.0).then_inc(const_c, 1)
            pool.wait_ge(const_c, 11 + HQ)
            g.memset(esel[MROW:MROW + 1, :, :].bitcast(F32), 0.0).then_inc(const_c, 1)
            pool.wait_ge(const_c, 12 + HQ)

            with pool.Fori(0, NQUAD) as qn:
                for s, (c, j) in enumerate(STEPS):
                    r = j - CT * c
                    if r >= 0:
                        for p in range(NPAIR):
                            pool.wait_ge(exp_done, ONE + (qn * NSTEP + s) * NPAIR + p + 1).then_inc(pool_waited, 1)
                            blk = Pb[s % 2][p][:, :, r * P:(r + 1) * P]
                            g.affine_select(out=blk, in_=blk, compare_op=ALU.is_ge, fill=0.0, base=0,
                                            pattern=[[0, 2], [1, P]], channel_multiplier=-1).then_inc(mask_done, 1)
                    if j == 3:
                        k = qn * NCH + c
                        cols = slice(c * CW, (c + 1) * CW)
                        pool.wait_ge(cum_in, (qn + 1) * 16)
                        pool.wait_ge(num_done, ONE + k)
                        g.tensor_tensor(SE[:], cum[:, T - 1:T].broadcast_to([P, CW]), cum[:, cols], ALU.subtract).then_inc(sub_done, 1)
                        pool.wait_ge(E_done, ONE + k + 1)
                        pool.wait_ge(sub_done, ONE + k + 1)
                        g.tensor_tensor(SE[:], SE[:], Eb[:], ALU.mult).then_inc(SE_done, 1)
                        pool.wait_ge(ost_done, ONE + k)
                        g.tensor_tensor(NE[:], later[:, cols], Eb[:], ALU.mult).then_inc(NE_done, 1)

        @block.scalar
        def _(act):
            a = nc.scalar
            for k in range(KT):
                act.wait_ge(T_full, k + 1)
                a.copy(wf_t[:, k, :], psT[k % 2][:]).then_inc(wf_done, 1)
            act.wait_ge(bias_in, (2 * KT + 1) * 16)
            with act.Fori(0, B) as b:
                for c in range(NCH):
                    n = b * NCH + c
                    act.wait_ge(P_full, ONE + n * NPU)
                    for k in range(KT):
                        act.wait_ge(T_full, KT + n * NTU + k + 1)
                        a.copy(xh[:, k, :], psT[k % 2][:]).then_inc(xh_done, 1)
                    for k in range(KT):
                        act.wait_ge(T_full, KT + n * NTU + KT + k + 1)
                        act.wait_ge(yl_done, ONE + n * KT + max(0, k - 1))
                        a.activation(yf[k % 2][:], psT[k % 2][:], ACT.Identity, bias=bet[:, k:k + 1],
                                     scale=gam[:, k:k + 1]).then_inc(yf_done, 1)
                    for k in range(2 * NQ):
                        act.wait_ge(P_full, ONE + n * NPU + k + 1)
                        act.wait_ge(st_out[k % 4], ONE + (n * 2 + k // 4) * 32)
                        a.copy(st_hi[k % 4][:], psP[k % 4][:]).then_inc(hi_done, 1)
                    act.wait_ge(vs_out, ONE + n * NQ * 16)
                    act.wait_ge(T_full, KT + n * NTU)
                    for j in range(CT):
                        act.wait_ge(P_full, ONE + n * NPU + 2 * NQ + j + 1)
                        a.copy(vs[:, j, :], psP[j % 4][:]).then_inc(vs_done, 1)
                    for j in range(CT):
                        act.wait_ge(zb_done, ONE + n * CT + j + 1)
                        act.wait_ge(gs_out[j % 2], ONE + (n * (CT // 2) + j // 2) * 16)
                        a.activation(gs[j % 2][:], zb[j % 2][:], ACT.Silu).then_inc(gs_done, 1)

            phase_a_over(act)
            with act.Fori(0, NQUAD) as qn:
                act.wait_ge(L_full, ONE + qn * NLU + 1)
                act.wait_ge(mrow_in, ONE + qn * 32)
                a.copy(mrow[:], psL[:, 0:P]).then_inc(mrow_done, 1)
                for s, (c, j) in enumerate(STEPS):
                    o = max(0, j - CT * c) * P
                    step = qn * NSTEP + s
                    act.wait_ge(pv_done, ONE + (step if s == 0 else step - 1))
                    act.wait_ge(sum_done, ONE + (step * NPAIR if s == 0 else (step - 1) * NPAIR))
                    for p in range(NPAIR):
                        act.wait_ge(S_full, step * NPAIR + p + 1)
                        a.activation(Pb[s % 2][p][:, :, o:], psS[p][:, :, o:], ACT.Exp, scale=SCALE).then_inc(exp_done, 1)
                    if j == 3:
                        act.wait_ge(L_full, ONE + qn * NLU + 2 * c + 2)
                        act.wait_ge(NE_done, ONE + qn * NCH + c)
                        a.activation(Eb[:], psL[:], ACT.Exp, scale=SCALE).then_inc(E_done, 1)

        @block.vector
        def _(dve):
            v = nc.vector
            dve.wait_ge(xt_in[0], 16)
            v.tensor_reduce(wabs[:], xt[0][:], AX.XY, ALU.add, apply_absolute_value=True).then_inc(wabs_done, 1)
            dve.wait_ge(wtot_done, 1)
            v.tensor_scalar(wsc[:, 0:1], psW[:, 0:1], 1.0 / (D * D), EPS, ALU.mult, ALU.add).then_inc(wprep, 1)
            dve.wait_ge(wprep, 1)
            v.tensor_scalar(wsc[:, 1:2], wsc[:, 0:1], 0.5, None, ALU.mult).then_inc(wprep, 1)
            v.tensor_scalar(wsc[:, 2:3], wsc[:, 0:1], -0.5, None, ALU.mult).then_inc(wprep, 1)
            dve.wait_ge(wprep, 3)
            v.tensor_scalar(zn[:], xt[0][:], wsc[:, 2:3], None, ALU.is_lt).then_inc(wprep, 1)
            dve.wait_ge(wprep, 4)
            for k in range(KT):
                v.scalar_tensor_tensor(out=vs[:, k, :], in0=xt[0][:, k, :], scalar=wsc[:, 1:2], in1=zn[:, k, :],
                                       op0=ALU.is_gt, op1=ALU.subtract).then_inc(tern_done, 1)
            dve.wait_ge(tern_done, KT)
            v.tensor_copy(wsc[:, 3:4], wsc[:, 2:3]).then_inc(xt_used, 1)
            for i in range(3):
                st = xt[(i + 1) % 2]
                dve.wait_ge(xt_in[(i + 1) % 2], 16 * ((i + 1) // 2 + 1))
                v.tensor_copy(w_hi[i][:], st[:]).then_inc(wprep, 1)
                dve.wait_ge(wprep, 5 + i)
                v.tensor_tensor(w_lo[i][:], st[:], w_hi[i][:].bitcast(F32), ALU.subtract).then_inc(xt_used, 1)

            def layernorm(n, i, src, dst, done, free):
                own = (2 * n + i) * 2 * CT
                for j in range(CT):
                    v.bn_stats(stats[:, j, :], src[:, j, :]).then_inc(ln_own, 1)
                dve.wait_ge(ln_own, own + CT).then_inc(dve_waited, 1)
                for j in range(CT):
                    v.bn_aggr(mv[i][:, j, :], stats[:, j, :]).then_inc(ln_own, 1)
                dve.wait_ge(ln_own, own + 2 * CT)
                v.tensor_scalar(ve[i][:], mv[i][:, :, 1], EPS, None, ALU.add).then_inc(ve_done, 1)
                dve.wait_ge(rstd_done, 2 * n + i + 1)
                dve.wait_ge(T_full, free)
                for j in range(CT):
                    ins = v.tensor_scalar(dst[:, j, :], src[:, j, :], mv[i][:, j, 0:1], rstd[i][:, j:j + 1],
                                          ALU.subtract, ALU.mult)
                ins.then_inc(done, 1)

            dve.wait_ge(bias_in, (2 * KT + 1) * 16)
            dve.wait_ge(const_a, 4)
            with dve.Fori(0, B) as b:
                for c in range(NCH):
                    n = b * NCH + c
                    dve.wait_ge(xt_in[c % 2], (3 + 2 * b + c // 2) * 16)
                    layernorm(n, 0, xt[c % 2], xn, xt_used, n * NTU if c else KT + n * NTU)
                    dve.wait_ge(xt_used, 4 + n + 1)
                    layernorm(n, 1, xn, zn, zn_done, n * NTU if c else KT + n * NTU)
                    dve.wait_ge(P_full, ONE + n * NPU)
                    for k in range(KT):
                        dve.wait_ge(xh_done, n * KT + k + 1)
                        v.tensor_tensor(xl[:, k, :], psT[k % 2][:], xh[:, k, :].bitcast(F32), ALU.subtract).then_inc(xl_done, 1)
                    for k in range(KT):
                        dve.wait_ge(yf_done, n * KT + k + 1)
                        v.tensor_copy(yh[:, k, :], yf[k % 2][:]).then_inc(yh_done, 1)
                        dve.wait_ge(yh_done, n * KT + k + 1)
                        v.tensor_tensor(yl[:, k, :], yf[k % 2][:], yh[:, k, :].bitcast(F32), ALU.subtract).then_inc(yl_done, 1)
                    for k in range(2 * NQ):
                        dve.wait_ge(hi_done, n * 2 * NQ + k + 1)
                        v.tensor_tensor(st_lo[k % 4][:], psP[k % 4][:], st_hi[k % 4][:].bitcast(F32), ALU.subtract).then_inc(lo_done, 1)

                    for j in range(CT):
                        dve.wait_ge(P_full, ONE + n * NPU + 3 * KT + j + 1)
                        dve.wait_ge(gs_done, ONE + n * CT + max(0, j - 1))
                        v.tensor_tensor(zb[j % 2][:], psP[j % 4][:], bias_b[:], ALU.add).then_inc(zb_done, 1)
                    for m in range(NQ):
                        dve.wait_ge(T_full, KT + n * NTU + 2 * KT + m + 1)
                        dve.wait_ge(cs_out[m], ONE + n * 16)
                        dve.wait_ge(carry_done, ONE + n * NQ)
                        v.tensor_tensor_scan(cs[m][:], psT[m % 2][:], zeros[:], 0.0 if c == 0 else carry[:, m:m + 1],
                                             ALU.add, ALU.add).then_inc(cs_done, 1)
                    for m in range(NQ):
                        dve.wait_ge(cs_done, ONE + n * NQ + m + 1)
                        v.tensor_copy(carry[:, m:m + 1], cs[m][:, CW - 1:CW]).then_inc(carry_done, 1)

            phase_a_over(dve)
            dve.wait_ge(const_c, 12 + HQ)
            with dve.Fori(0, NQUAD) as qn:
                for k in range(NMB):
                    segs, slot, step = MAXB[k % len(MAXB)]
                    first = (k // len(MAXB)) * NT * CT + slot
                    w, ns = segs[0][2], len(segs)
                    dve.wait_ge(M_full, qn * NMB + k + 1)
                    flat = mx[:].rearrange("p a b -> p (a b)")
                    v.tensor_reduce(flat[:, first:first + step * (ns - 1) + 1:step],
                                    psM[k % 2][:, 0:ns * w].rearrange("p (a b) -> p a b", a=ns), AX.X, ALU.max).then_inc(mx_done, 1)
                dve.wait_ge(mx_done, ONE + (qn + 1) * NMB)
                v.tensor_reduce(mred[:], mx[:], AX.X, ALU.max).then_inc(mred_done, 1)
                dve.wait_ge(mred_done, 2 * qn + 1)
                v.tensor_tensor(mmax[:], mred[:], zrow[:].rearrange("p a b -> p (a b)"), ALU.max).then_inc(mred_done, 1)
                dve.wait_ge(mred_done, 2 * qn + 2)
                v.tensor_scalar(mneg[:, 0:HQ * NT], mmax[:], -1.0, None, ALU.mult).then_inc(mneg_done, 1)
                v.tensor_scalar(mneg[:, HQ * NT:], mred[:], 0.0, -1.0, ALU.max, ALU.mult).then_inc(mneg_done, 1)

                def finish(c):
                    k = qn * NCH + c
                    dve.wait_ge(L_full, ONE + qn * NLU + 2 * c + 3)
                    dve.wait_ge(NE_done, ONE + k + 1)
                    v.tensor_tensor(NE[:], psL[:], NE[:], ALU.add).then_inc(add_done, 1)
                    dve.wait_ge(add_done, ONE + k + 1)
                    v.reciprocal(NE[:], NE[:]).then_inc(den_done, 1)
                    dve.wait_ge(den_done, k + 1)
                    dve.wait_ge(num_done, ONE + k + 1)
                    dve.wait_ge(ost_out[c % 2], ONE + (qn * (NCH // 2) + c // 2) * 16)
                    v.tensor_tensor(ost[c % 2][:], num[:], NE[:], ALU.mult).then_inc(ost_done, 1)

                for s, (c, j) in enumerate(STEPS):
                    r = j - CT * c
                    o = max(0, r) * P
                    step = qn * NSTEP + s
                    for p in range(NPAIR):
                        if r >= 0:
                            dve.wait_ge(mask_done, qn * NT * NPAIR + (CT * c + r) * NPAIR + p + 1)
                        else:
                            dve.wait_ge(exp_done, ONE + step * NPAIR + p + 1)
                        A = acc[c % 2][p]
                        if j == 0:
                            dve.wait_ge(L_full, ONE + (qn * NLU + (2 * (c - 2) + 3 if c >= 2 else 0)))
                            v.tensor_copy(A[:], Pb[s % 2][p][:]).then_inc(sum_done, 1)
                        else:
                            dve.wait_ge(sum_done, ONE + (step - 1) * NPAIR + p + 1)
                            v.tensor_tensor(A[:, :, o:], A[:, :, o:], Pb[s % 2][p][:, :, o:], ALU.add).then_inc(sum_done, 1)
                    if j == 0 and c > 0:
                        finish(c - 1)
                    if s == last_step[c]:
                        dve.wait_ge(pv_done, ONE + step + 1)
                        dve.wait_ge(SE_done, qn * NCH + c + 1)
                        v.tensor_tensor(num[:], psO[:], SE[:], ALU.add).then_inc(num_done, 1)
                finish(NCH - 1)

            dve.wait_ge(L_full, ONE + NQUAD * NLU)
            attention_over(dve)
            with dve.Fori(0, B) as b:
                for c in range(NCH):
                    n = b * NCH + c
                    dve.wait_ge(d_in[c % 2], (b * 2 + c // 2 + 1) * 48)
                    dve.wait_ge(oo_out[c % 2], ONE + (b * 2 + c // 2) * 16)
                    for j in range(CT):
                        dve.wait_ge(D_full, n * CT + j + 1)
                        v.tensor_tensor(sg[j % 2][:], psD[4 * (c % 2) + j][:], gr[c % 2][:, j, :], ALU.mult).then_inc(sg_done, 1)
                        dve.wait_ge(sg_done, ONE + n * CT + j + 1)
                        v.tensor_tensor(oo[c % 2][:, j, :], sg[j % 2][:], xr[c % 2][:, j, :], ALU.add).then_inc(oo_done, 1)

        @block.tensor
        def _(pe):
            t = nc.tensor
            pe.wait_ge(const_a, 4)
            pe.wait_ge(wabs_done, 1)
            t.matmul(psW[:, 0:1], ones[:], wabs[:], start=True, stop=True).then_inc(wtot_done, 1)
            pe.wait_ge(tern_done, KT)
            for k in range(KT):
                if k >= 2:
                    pe.wait_ge(wf_done, k - 1)
                for i in range(KT):
                    ins = t.transpose(psT[k % 2][:, i * P:(i + 1) * P], vs[:, i, k * P:(k + 1) * P], ident[:])
                ins.then_inc(T_full, 1)
            pe.wait_ge(wf_done, KT)

            with pe.Fori(0, B) as b:
                for c in range(NCH):
                    n = b * NCH + c

                    def transposes(k, src, at):
                        for j in range(CT):
                            ins = t.transpose(psT[k % 2][:, j * P:(j + 1) * P], src[:, j, at * P:(at + 1) * P], ident[:])
                        ins.then_inc(T_full, 1)

                    pe.wait_ge(xt_used, 4 + n + 1)
                    for k in range(KT):
                        if k < 2:
                            pe.wait_ge(cs_done, ONE + n * NQ)
                        else:
                            pe.wait_ge(xl_done, n * KT + k - 1)
                        transposes(k, xn, k)
                    pe.wait_ge(zn_done, n + 1)
                    for k in range(KT):
                        if k < 2:
                            pe.wait_ge(xl_done, n * KT + KT - 1 + k)
                        else:
                            pe.wait_ge(yf_done, n * KT + k - 1)
                        transposes(k, zn, k)
                    pe.wait_ge(xl_done, (n + 1) * KT)
                    for i in range(2):
                        for m in range(NQ):
                            if i == 0:
                                pe.wait_ge(zb_done, ONE + n * CT)
                            else:
                                pe.wait_ge(lo_done, n * 2 * NQ + m + 1)
                            cols = slice(m * P, (m + 1) * P)
                            parts = [(w_hi[i], xh), (w_hi[i], xl), (w_lo[i], xh)]
                            for a, (w, xx) in enumerate(parts):
                                for k in range(KT):
                                    ins = t.matmul(psP[m][:], w[:, k, cols], xx[:, k, :], start=(a + k == 0),
                                                   stop=(a == 2 and k == KT - 1))
                            ins.then_inc(P_full, 1)
                    for j in range(CT):
                        pe.wait_ge(lo_done, n * 2 * NQ + NQ + j + 1)
                        cols = slice(j * P, (j + 1) * P)
                        parts = [(xh, w_hi[2]), (xl, w_hi[2]), (xh, w_lo[2])]
                        for a, (xx, w) in enumerate(parts):
                            for k in range(KT):
                                ins = t.matmul(psP[j][:], xx[:, k, cols], w[:, k, :], start=(a + k == 0),
                                               stop=(a == 2 and k == KT - 1))
                        ins.then_inc(P_full, 1)
                    pe.wait_ge(yl_done, ONE + (n + 1) * KT)
                    for j in range(CT):
                        pe.wait_ge(vs_done, n * CT + j + 1)
                        cols = slice(j * P, (j + 1) * P)
                        for a, yy in enumerate((yh, yl)):
                            for k in range(KT):
                                ins = t.matmul(psP[j][:], yy[:, k, cols], wf_t[:, k, :], start=(a + k == 0),
                                               stop=(a == 1 and k == KT - 1))
                        ins.then_inc(P_full, 1)
                    for m in range(NQ):
                        if m < 2:
                            pe.wait_ge(yf_done, n * KT + KT - 1 + m)
                        else:
                            pe.wait_ge(cs_done, ONE + n * NQ + m - 1)
                        transposes(m, vs, m)

            phase_a_over(pe)
            pe.wait_ge(const_c, 12 + HQ)
            with pe.Fori(0, NQUAD // 2) as i:
                for par in range(2):
                    qn = 2 * i + par
                    Q, K, V = Qs[par], Ks[par], Vs[par]
                    pe.wait_ge(kq_in[par], (i + 1) * 96)
                    for k in range(NMB):
                        h = k // len(MAXB)
                        segs, _, _ = MAXB[k % len(MAXB)]
                        pe.wait_ge(mx_done, ONE + qn * NMB + max(0, k - 1))
                        for z, (tile, k0, w) in enumerate(segs):
                            at = z * w
                            diag = k0 + w == (tile + 1) * P
                            ins = t.matmul(psM[k % 2][:, at:at + w], Q[0:STACK, h, tile * P:(tile + 1) * P],
                                           K[0:STACK, h, k0:k0 + w], start=True, stop=not diag)
                            if diag:
                                ins = t.matmul(psM[k % 2][:, at + w - P:at + w], identb[:], negm[:], start=False, stop=True)
                        ins.then_inc(M_full, 1)
                    pe.wait_ge(mneg_done, 2 * qn + 2)
                    pe.wait_ge(add_done, ONE + qn * NCH)
                    t.transpose(psL[:, 0:P], mneg[:].bitcast(F32), ident[:]).then_inc(L_full, 1)
                    pe.wait_ge(v_in[par], (i + 1) * 16)
                    pe.wait_ge(mrow_in, ONE + (qn + 1) * 32)

                    def scores(s):
                        c, j = STEPS[s]
                        o = max(0, j - CT * c) * P
                        step = qn * NSTEP + s
                        for p in range(NPAIR):
                            pe.wait_ge(exp_done, ONE + (step * NPAIR if s == 0 else step * NPAIR + p - 1))
                            for e in range(2):
                                h = 2 * p + e
                                ins = t.matmul(psS[p][:, e, o:], K[0:MROW + 1, h, j * P:(j + 1) * P],
                                               Q[0:MROW + 1, h, c * CW + o:(c + 1) * CW], start=True, stop=True)
                            ins.then_inc(S_full, 1)

                    def values(s):
                        c, j = STEPS[s]
                        r = j - CT * c
                        o = max(0, r) * P
                        step = qn * NSTEP + s
                        if j == 0:
                            pe.wait_ge(num_done, ONE + qn * NCH + c)
                        for h in range(HQ):
                            p = h // 2
                            if h % 2 == 0 and r >= 0:
                                pe.wait_ge(mask_done, qn * NT * NPAIR + (CT * c + r) * NPAIR + p + 1)
                            elif h % 2 == 0:
                                pe.wait_ge(exp_done, ONE + step * NPAIR + p + 1)
                            hc = slice(h * DH, (h + 1) * DH)
                            ins = t.matmul(psO[hc, o:], V[:, j, hc], Pb[s % 2][p][:, h % 2, o:],
                                           start=(j == 0), stop=(s == last_step[c]), skip_group_check=True)
                        ins.then_inc(pv_done, 1)

                    def row_sums(c):
                        pe.wait_ge(sum_done, ONE + (qn * NSTEP + last_step[c] + 1) * NPAIR)
                        pe.wait_ge(E_done, ONE + qn * NCH + c + 1)
                        for h in range(HQ):
                            ins = t.matmul(psL[h * DH:(h + 1) * DH, :], ones[:, 0:DH], acc[c % 2][h // 2][:, h % 2, :],
                                           start=True, stop=True)
                        ins.then_inc(L_full, 1)

                    def spread_max(c):
                        if c == 0:
                            pe.wait_ge(mrow_done, qn + 1)
                        else:
                            pe.wait_ge(add_done, ONE + qn * NCH + c)
                        for h in range(HQ):
                            ins = t.matmul(psL[:], esel[0:M0ROW + 1, h, :], Q[0:M0ROW + 1, h, c * CW:(c + 1) * CW],
                                           start=(h == 0), stop=(h == HQ - 1))
                        ins.then_inc(L_full, 1)

                    scores(0)
                    for s, (c, j) in enumerate(STEPS):
                        if s + 1 < NSTEP:
                            scores(s + 1)
                        values(s)
                        if j == 0 and c > 0:
                            row_sums(c - 1)
                        if j == 2:
                            spread_max(c)
                    row_sums(NCH - 1)

            attention_over(pe)
            pe.wait_ge(ost_done, ONE + NQUAD * NCH)
            pe.wait_ge(wo_in, 16)
            with pe.Fori(0, B) as b:
                for c in range(NCH):
                    n = b * NCH + c
                    pe.wait_ge(d_in[c % 2], (b * 2 + c // 2 + 1) * 48)
                    for j in range(CT):
                        pe.wait_ge(sg_done, ONE + (n * CT if c == 0 else (n - 1) * CT))
                        for k in range(KT):
                            ins = t.matmul(psD[4 * (c % 2) + j][:], ac[c % 2][:, k, j * P:(j + 1) * P], wo[:, k, :],
                                           start=(k == 0), stop=(k == KT - 1))
                        ins.then_inc(D_full, 1)


_INS = ["L0_attn_x", "L0_attn_Wq", "L0_attn_Wk", "L0_attn_Wv", "L0_attn_Wo", "L0_ffn_weight", "L0_ffn_bias",
        "L0_ffn_ln_gamma", "L0_ffn_ln_beta"]


def kernel(**inputs):
    import numpy as np
    import concourse.bacc as bacc
    from concourse.bass_utils import run_bass_kernel_spmd

    nc = bacc.Bacc("TRN2", target_bir_lowering=False, num_devices=1)
    arrays, args = {}, []
    for name in _INS:
        a = np.ascontiguousarray(inputs[name])
        arrays[f"in_{name}"] = a
        args.append(nc.dram_tensor(f"in_{name}", a.shape, mybir.dt.from_np(a.dtype), kind="ExternalInput").ap())
    out = nc.dram_tensor("out_0", (B, T, D), F32, kind="ExternalOutput").ap()
    build(nc, *args, out)
    r = run_bass_kernel_spmd(nc, [arrays], core_ids=[0])
    return r.results[0]["out_0"]
```

```python
from contextlib import ExitStack

import concourse.bass as bass
from concourse import mybir

F32 = mybir.dt.float32
F32R = mybir.dt.float32r
BF16 = mybir.dt.bfloat16
F16 = mybir.dt.float16
ACT = mybir.ActivationFunctionType
ALU = mybir.AluOpType
AX = mybir.AxisListType

P = 128
B, T, D, H = 2, 2048, 512, 16
DH = D // H
KT = D // P
HQ = P // DH
NQ = H // HQ
NQUAD = B * NQ
CW = 512
NCH = T // CW
CT = CW // P
NT = T // P
SCALE = float(T) ** -0.5
EPS = 1e-5
BIG = 1e30
STACK = 3 * DH
MROW = STACK
NSTEP = sum(CT * c + CT for c in range(NCH))
STEPS = [(c, j) for c in range(NCH) for j in range(CT * c + CT)]
NPAIR = HQ // 2
START = 4
MAX_END = 36


def max_banks():
    banks = []
    for i in range(NT):
        for f in range((i + 1) // CT):
            banks.append(([(i, f * CW, CW)], i * CT + f, 1))
    for r in range(1, CT):
        w = r * P
        per = CW // w
        tiles = [i for i in range(NT) if (i + 1) % CT == r]
        for a in range(0, len(tiles), per):
            part = tiles[a:a + per]
            slots = [i * CT + (i + 1) // CT for i in part]
            banks.append(([(i, (i + 1) // CT * CW, w) for i in part], slots[0], CT * CT + 1))
    return banks


MAXB = sorted(((max(i for i, _, _ in segs), h, segs, h * NT * CT + slot, step)
               for h in range(HQ) for segs, slot, step in max_banks()), key=lambda m: m[0] // (NT // 2))
NMB = len(MAXB)
NLOW = sum(m[0] < NT // 2 for m in MAXB)


def width(s):
    c, j = STEPS[s]
    return CW - max(0, j - CT * c) * P


def max_share(s):
    whole = sum(width(i) for i in range(MAX_END))
    def upto(s):
        return NMB * sum(width(i) for i in range(min(s, MAX_END))) // whole
    return range(upto(s), upto(s + 1))


def ring(s):
    return sum(1 for c, j in STEPS[:s] if j) % 2


def ring_before(s):
    with_ring = [i for i in range(-NSTEP, s) if STEPS[i % NSTEP][1] and ring(i % NSTEP) == ring(s)]
    return with_ring[-1]


def sums_before(s):
    return NPAIR * sum(1 for c, j in STEPS[:s] if j % 2)


NSUM = sums_before(NSTEP)


def build(nc, x, Wq, Wk, Wv, Wo, Wf, bias, gamma, beta, out):
    top = ExitStack()
    with top:
        def sem(name):
            return top.enter_context(nc.semaphore(name))

        def sbuf(stack, name, shape, dt):
            return stack.enter_context(nc.sbuf_tensor(name, shape, dt))

        def psum(stack, name, shape):
            return stack.enter_context(nc.psum_tensor(name, shape, F32))

        q_hi = nc.dram_tensor("q_hi", [B * D, T], F32).ap()
        q_lo = nc.dram_tensor("q_lo", [B * D, T], F32).ap()
        k_hi = nc.dram_tensor("k_hi", [B * D, T], F32).ap()
        k_lo = nc.dram_tensor("k_lo", [B * D, T], F32).ap()
        v_quad = nc.dram_tensor("v_quad", [NQUAD * P, NT * P], F32).ap()
        v_cum = nc.dram_tensor("v_cum", [B * D, T], F32).ap()
        m_rows = nc.dram_tensor("m_rows", [NQUAD * HQ, T], F32).ap()
        gate = nc.dram_tensor("gate", [B * T, D], F32).ap()
        att_t = nc.dram_tensor("att_t", [B * D, T], F32).ap()

        ident = sbuf(top, "ident", [P, P], F32)
        ones = sbuf(top, "ones", [P, P], F32)

        pa = ExitStack()
        w_hi = [sbuf(pa, f"w_hi{i}", [P, KT, D], F32R) for i in range(3)]
        w_lo = [sbuf(pa, f"w_lo{i}", [P, KT, D], F32R) for i in range(3)]
        wf_t = sbuf(pa, "wf_t", [P, KT, D], F32R)
        xt = [sbuf(pa, f"xt{i}", [P, CT, D], F32) for i in range(2)]
        xn = sbuf(pa, "xn", [P, CT, D], F32)
        zn = sbuf(pa, "zn", [P, CT, D], F32)
        xh = sbuf(pa, "xh", [P, KT, CW], F32R)
        xl = sbuf(pa, "xl", [P, KT, CW], F32R)
        yf = [sbuf(pa, f"yf{i}", [P, CW], F32) for i in range(2)]
        yh = sbuf(pa, "yh", [P, KT, CW], F32R)
        yl = sbuf(pa, "yl", [P, KT, CW], F32R)
        st_hi = [sbuf(pa, f"st_hi{i}", [P, CW], F32R) for i in range(4)]
        st_lo = [sbuf(pa, f"st_lo{i}", [P, CW], F32R) for i in range(4)]
        vs = sbuf(pa, "vs", [P, CT, D], F32)
        cs = [sbuf(pa, f"cs{i}", [P, CW], F32) for i in range(NQ)]
        carry = sbuf(pa, "carry", [P, NQ], F32)
        zb = [sbuf(pa, f"zb{i}", [P, D], F32) for i in range(2)]
        gs = [sbuf(pa, f"gs{i}", [P, D], F32) for i in range(2)]
        bias_b = sbuf(pa, "bias_b", [P, D], F32)
        zeros = sbuf(pa, "zeros", [P, CW], F32)
        gam = sbuf(pa, "gam", [P, KT], F32)
        bet = sbuf(pa, "bet", [P, KT], F32)
        stats = sbuf(pa, "stats", [P, CT, 6], F32)
        mv = [sbuf(pa, f"mv{i}", [P, CT, 2], F32) for i in range(2)]
        ve = [sbuf(pa, f"ve{i}", [P, CT], F32) for i in range(2)]
        rstd = [sbuf(pa, f"rstd{i}", [P, CT], F32) for i in range(2)]
        mhalf = sbuf(pa, "mhalf", [P, CT], F32)
        wabs = sbuf(pa, "wabs", [P, 1], F32)
        wsc = sbuf(pa, "wsc", [P, 4], F32)
        psT = [psum(pa, f"psT{i}", [P, CW]) for i in range(2)]
        psP = [psum(pa, f"psP{i}", [P, CW]) for i in range(4)]
        psW = psum(pa, "psW", [P, CW])
        pa.close()

        pc = ExitStack()
        Qs = [sbuf(pc, f"Qs{i}", [P, HQ, T], F32R) for i in range(2)]
        Ks = [sbuf(pc, f"Ks{i}", [P, HQ, T], F32R) for i in range(2)]
        Vs = [sbuf(pc, f"Vs{i}", [P, NT, P], F32) for i in range(2)]
        Pb = [[sbuf(pc, f"Pb{i}_{p}", [P, 2, CW], F32) for p in range(NPAIR)] for i in range(2)]
        acc = [[sbuf(pc, f"acc{i}_{p}", [P, 2, CW], F32) for p in range(NPAIR)] for i in range(2)]
        cum = sbuf(pc, "cum", [P, T], F32)
        later = sbuf(pc, "later", [P, T], F16)
        E = sbuf(pc, "E", [P, T], F32)
        tot = sbuf(pc, "tot", [P, 1], F32)
        num = sbuf(pc, "num", [P, CW], F32)
        ost = [sbuf(pc, f"ost{i}", [P, CW], F32) for i in range(2)]
        identb = sbuf(pc, "identb", [P, P], BF16)
        negm = sbuf(pc, "negm", [P, P], BF16)
        zrow = sbuf(pc, "zrow", [P, HQ, NT], F32)
        mx = sbuf(pc, "mx", [P, HQ * NT, CT], F32)
        mred = sbuf(pc, "mred", [P, HQ * NT], F32)
        mmax = sbuf(pc, "mmax", [P, HQ * NT], F32)
        mneg = sbuf(pc, "mneg", [P, 2 * HQ * NT], F32R)
        mrow = [sbuf(pc, f"mrow{i}", [HQ * NT, P], F32R) for i in range(2)]
        psS = [psum(pc, f"psS{i}", [P, 2, CW]) for i in range(2)]
        psM = [psum(pc, f"psM{i}", [P, CW]) for i in range(2)]
        psO = psum(pc, "psO", [P, CW])
        psL = psum(pc, "psL", [P, CW])
        pc.close()

        pd = ExitStack()
        wo = sbuf(pd, "wo", [P, KT, D], F32)
        ac = [sbuf(pd, f"ac{i}", [P, KT, CW], F32) for i in range(2)]
        xr = [sbuf(pd, f"xr{i}", [P, CT, D], F32) for i in range(2)]
        gr = [sbuf(pd, f"gr{i}", [P, CT, D], F32) for i in range(2)]
        oo = [sbuf(pd, f"oo{i}", [P, CT, D], F32) for i in range(2)]
        sg = [sbuf(pd, f"sg{i}", [P, D], F32) for i in range(2)]
        psD = [psum(pd, f"psD{i}", [P, D]) for i in range(8)]
        pd.close()

        const_a = sem("const_a")
        bias_in = sem("bias_in")
        xt_in = [sem(f"xt_in{i}") for i in range(2)]
        xt_used = sem("xt_used")
        wabs_done = sem("wabs_done")
        wtot_done = sem("wtot_done")
        wprep = sem("wprep")
        tern_done = sem("tern_done")
        wf_done = sem("wf_done")
        T_full = sem("T_full")
        P_full = sem("P_full")
        ln_own = sem("ln_own")
        dve_waited = sem("dve_waited")
        ve_done = sem("ve_done")
        rstd_done = sem("rstd_done")
        zn_done = sem("zn_done")
        xh_done = sem("xh_done")
        xl_done = sem("xl_done")
        yf_done = sem("yf_done")
        yh_done = sem("yh_done")
        yl_done = sem("yl_done")
        hi_done = sem("hi_done")
        lo_done = sem("lo_done")
        st_out = [sem(f"st_out{i}") for i in range(4)]
        vs_done = sem("vs_done")
        vs_out = sem("vs_out")
        cs_done = sem("cs_done")
        carry_done = sem("carry_done")
        cs_out = [sem(f"cs_out{i}") for i in range(NQ)]
        zb_done = sem("zb_done")
        gs_done = sem("gs_done")
        gs_out = [sem(f"gs_out{i}") for i in range(2)]
        const_c = sem("const_c")
        kq_low = [sem(f"kq_low{i}") for i in range(2)]
        kq_high = [sem(f"kq_high{i}") for i in range(2)]
        v_in = [sem(f"v_in{i}") for i in range(2)]
        cum_in = [sem(f"cum_in{c}") for c in range(NCH)]
        M_full = sem("M_full")
        mx_done = sem("mx_done")
        mred_done = sem("mred_done")
        mneg_done = sem("mneg_done")
        mrow_done = sem("mrow_done")
        mrow_in = sem("mrow_in")
        m0_out = sem("m0_out")
        e_in = [sem(f"e_in{c}") for c in range(NCH)]
        S_full = sem("S_full")
        exp_done = sem("exp_done")
        mask_done = sem("mask_done")
        pool_waited = sem("pool_waited")
        pe_waited = sem("pe_waited")
        sp_waited = sem("sp_waited")
        pv_done = sem("pv_done")
        sum_done = sem("sum_done")
        L_full = sem("L_full")
        E_done = sem("E_done")
        sub_done = sem("sub_done")
        SE_done = sem("SE_done")
        NE_done = sem("NE_done")
        num_done = sem("num_done")
        add_done = sem("add_done")
        rec_done = sem("rec_done")
        ost_done = sem("ost_done")
        ost_out = [sem(f"ost_out{i}") for i in range(2)]
        wo_in = sem("wo_in")
        d_in = [sem(f"d_in{i}") for i in range(2)]
        D_full = sem("D_full")
        sg_done = sem("sg_done")
        oo_done = sem("oo_done")
        oo_out = [sem(f"oo_out{i}") for i in range(2)]

        x_v = x.rearrange("b (c j p) d -> (b c) p j d", p=P, j=CT)
        out_v = out.rearrange("b (c j p) d -> (b c) p j d", p=P, j=CT)
        gate_t = gate.rearrange("(n p) d -> n p d", p=P)
        gate_v = gate.rearrange("(n j p) d -> n p j d", p=P, j=CT)
        w_q, w_k, w_v, w_o, w_f = (w.rearrange("(k p) n -> p k n", p=P) for w in (Wq, Wk, Wv, Wo, Wf))
        NTU = 3 * KT
        NPU = 3 * KT + CT
        NCHUNK = B * NCH
        last_step = [STEPS.index((c, CT * c + CT - 1)) for c in range(NCH)]

        credited = [mrow_done, m0_out, P_full, yl_done, vs_out, gs_done, cs_done, zb_done, carry_done, num_done, ost_done, add_done, L_full, mrow_in, pv_done, sum_done, SE_done, NE_done, exp_done, mx_done, sub_done, oo_done, sg_done, E_done,
                    *st_out, *gs_out, *cs_out, *ost_out, *oo_out]

        block = top.enter_context(nc.Block())

        def phase_a_over(eng):
            for s in range(4):
                eng.wait_ge(st_out[s], START + NCHUNK * 2 * 32)
            eng.wait_ge(vs_out, START + NCHUNK * NQ * 16)
            for m in range(NQ):
                eng.wait_ge(cs_out[m], START + NCHUNK * 16)
            for s in range(2):
                eng.wait_ge(gs_out[s], START + NCHUNK * (CT // 2) * 16)
            eng.wait_ge(carry_done, START + NCHUNK * NQ)
            eng.wait_ge(T_full, KT + NCHUNK * NTU)
            eng.wait_ge(P_full, START + NCHUNK * NPU)

        def attention_over(eng):
            for s in range(2):
                eng.wait_ge(ost_out[s], START + NQUAD * NCH // 2 * 16)
            eng.wait_ge(L_full, START + NQUAD * NCH)
            eng.wait_ge(NE_done, START + NQUAD * NCH)
            eng.wait_ge(ost_done, START + NQUAD * NCH)

        def quads(eng, body):
            with eng.Fori(0, NQUAD // 2 - 1) as i:
                body(2 * i, 0, True, True)
                body(2 * i + 1, 1, True, True)
            body(NQUAD - 2, 0, True, False)
            body(NQUAD - 1, 1, False, False)

        @block.sync
        def _(sp):
            sp.dma_start(xt[0][:], w_f).then_inc(xt_in[0], 16)
            sp.dma_start(xt[1][:], w_q).then_inc(xt_in[1], 16)
            for s in credited:
                sp.sem_inc(s, START)
            for k in range(KT):
                sp.dma_start(gam[:, k:k + 1], gamma.rearrange("(k p u) -> k p u", p=P, u=1)[k]).then_inc(bias_in, 16)
                sp.dma_start(bet[:, k:k + 1], beta.rearrange("(k p u) -> k p u", p=P, u=1)[k]).then_inc(bias_in, 16)
            sp.dma_start(bias_b[:], bias.rearrange("(u n) -> u n", u=1).broadcast_to([P, D])).then_inc(bias_in, 16)
            sp.wait_ge(xt_used, 1)
            sp.dma_start(xt[0][:], w_k).then_inc(xt_in[0], 16)
            sp.wait_ge(xt_used, 2)
            sp.dma_start(xt[1][:], w_v).then_inc(xt_in[1], 16)

            with sp.Fori(0, B) as b:
                for c in range(NCH):
                    n = b * NCH + c
                    if c == 0:
                        sp.wait_ge(xt_used, n + 3)
                        sp.dma_start(xt[0][:], x_v[n]).then_inc(xt_in[0], 16)
                    if c < NCH - 1:
                        sp.wait_ge(xt_used, n + 4)
                        sp.dma_start(xt[(c + 1) % 2][:], x_v[n + 1]).then_inc(xt_in[(c + 1) % 2], 16)
                    cols = slice(c * CW, (c + 1) * CW)
                    for k in range(2 * NQ):
                        hi, lo = (q_hi, q_lo) if k < NQ else (k_hi, k_lo)
                        rows = bass.ds(b * D + (k % NQ) * P, P)
                        sp.wait_ge(hi_done, n * 2 * NQ + k + 1)
                        sp.dma_start(hi[rows, cols], st_hi[k % 4][:].bitcast(F32)).then_inc(st_out[k % 4], 16)
                        sp.wait_ge(lo_done, n * 2 * NQ + k + 1)
                        sp.dma_start(lo[rows, cols], st_lo[k % 4][:].bitcast(F32)).then_inc(st_out[k % 4], 16)
                    sp.wait_ge(vs_done, (n + 1) * CT)
                    for m in range(NQ):
                        sp.dma_start(v_quad[bass.ds(b * D + m * P, P), cols].rearrange("p (j n) -> p j n", n=P),
                                     vs[:, :, m * P:(m + 1) * P]).then_inc(vs_out, 16)
                    for j in range(CT):
                        sp.wait_ge(gs_done, START + n * CT + j + 1)
                        sp.dma_start(gate_t[n * CT + j], gs[j % 2][:]).then_inc(gs_out[j % 2], 16)
                    for m in range(NQ):
                        sp.wait_ge(cs_done, START + n * NQ + m + 1)
                        sp.dma_start(v_cum[bass.ds(b * D + m * P, P), cols], cs[m][:]).then_inc(cs_out[m], 16)

            phase_a_over(sp)

            def load_half(qn, par, half):
                cols = slice(half * T // 2, (half + 1) * T // 2)

                def heads(a):
                    return a[bass.ds(qn * P, P), cols].rearrange("(h d) t -> d h t", d=DH)
                into = (kq_low, kq_high)[half][par]
                for g, (qa, ka) in enumerate(((q_hi, k_hi), (q_lo, k_hi), (q_hi, k_lo))):
                    rows = slice(g * DH, (g + 1) * DH)
                    sp.dma_start(Qs[par][rows, :, cols].bitcast(F32), heads(qa)).then_inc(into, 16)
                    sp.dma_start(Ks[par][rows, :, cols].bitcast(F32), heads(ka)).then_inc(into, 16)

            def load_values(qn, par):
                sp.dma_start(Vs[par][:], v_quad[bass.ds(qn * P, P), :].rearrange("p (j n) -> p j n", n=P)).then_inc(v_in[par], 16)

            def store_maxima(m, par):
                sp.wait_ge(mrow_done, START + 2 * m + 1)
                sp.dma_start(Qs[par][MROW:MROW + 1, :, :].bitcast(F32), mrow[0][:].bitcast(F32)).then_inc(mrow_in, 16)
                sp.wait_ge(mrow_done, START + 2 * m + 2)
                sp.dma_start(m_rows[bass.ds(m * HQ, HQ), :].rearrange("h (i p) -> (h i) p", p=P), mrow[1][:].bitcast(F32)).then_inc(m0_out, 16)

            def chunk_sums(m, c):
                cols = slice(c * CW, (c + 1) * CW)
                sp.wait_ge(SE_done, START + (m - 1) * NCH + c + 1)
                sp.wait_ge(num_done, START + (m - 1) * NCH + c + 1)
                sp.dma_start(cum[:, cols], v_cum[bass.ds(m * P, P), cols]).then_inc(cum_in[c], 16)
                if c == 0:
                    sp.wait_ge(sub_done, START + m * NCH)
                    sp.dma_start(tot[:], v_cum[bass.ds(m * P, P), T - 1:T],
                                 allow_slow_non_contiguous=True).then_inc(cum_in[c], 16)
                sp.wait_ge(add_done, START + (m - 1) * NCH + c + 1)
                sp.wait_ge(m0_out, START + (m + 1) * 16)
                for h in range(HQ):
                    sp.dma_start(E[h * DH:(h + 1) * DH, cols],
                                 m_rows[bass.ds(m * HQ + h, 1), cols].broadcast_to([DH, CW])).then_inc(e_in[c], 16)

            for half in range(2):
                load_half(0, 0, half)
            load_values(0, 0)
            for half in range(2):
                load_half(1, 1, half)
            load_values(1, 1)
            store_maxima(0, 0)
            for c in range(NCH - 1):
                chunk_sums(0, c)

            def quad(qn, par, more, load):
                chunk_sums(qn, NCH - 1)
                for c in range(NCH - 1):
                    sp.wait_ge(ost_done, START + qn * NCH + c + 1).then_inc(sp_waited, 1)
                    sp.dma_start(att_t[bass.ds(qn * P, P), c * CW:(c + 1) * CW], ost[c % 2][:]).then_inc(ost_out[c % 2], 16)
                if load:
                    sp.wait_ge(pv_done, START + qn * NSTEP + STEPS.index((NCH - 1, NT // 2)))
                    load_half(qn + 2, par, 0)
                if more:
                    store_maxima(qn + 1, 1 - par)
                    for c in range(NCH - 1):
                        chunk_sums(qn + 1, c)
                if load:
                    sp.wait_ge(pv_done, START + (qn + 1) * NSTEP)
                    load_half(qn + 2, par, 1)
                    load_values(qn + 2, par)
                sp.wait_ge(ost_done, START + (qn + 1) * NCH)
                sp.dma_start(att_t[bass.ds(qn * P, P), (NCH - 1) * CW:], ost[(NCH - 1) % 2][:]).then_inc(ost_out[(NCH - 1) % 2], 16)

            quads(sp, quad)
            attention_over(sp)
            sp.dma_start(wo[:], w_o).then_inc(wo_in, 16)

            with sp.Fori(0, B) as b:
                for c in range(NCH):
                    n = b * NCH + c
                    if c == 0:
                        loads = (0, 1)
                    elif c < NCH - 1:
                        loads = (c + 1,)
                    else:
                        loads = ()
                    for l in loads:
                        m = b * NCH + l
                        sp.wait_ge(oo_done, START + ((b * NCH if l < 2 else m - 1) * CT))
                        rows = bass.ds(b * D, D)
                        sp.dma_start(ac[l % 2][:], att_t[rows, l * CW:(l + 1) * CW].rearrange("(k p) w -> p k w", p=P)).then_inc(d_in[l % 2], 16)
                        sp.dma_start(xr[l % 2][:], x_v[m]).then_inc(d_in[l % 2], 16)
                        sp.dma_start(gr[l % 2][:], gate_v[m]).then_inc(d_in[l % 2], 16)
                    sp.wait_ge(oo_done, START + (n + 1) * CT)
                    sp.dma_start(out_v[n], oo[c % 2][:]).then_inc(oo_out[c % 2], 16)
            for s in range(2):
                sp.wait_ge(oo_out[s], START + NCHUNK // 2 * 16)

        @block.gpsimd
        def _(pool):
            g = nc.gpsimd
            g.memset(ones[:], 1.0).then_inc(const_a, 1)
            g.memset(zeros[:], 0.0).then_inc(const_a, 1)
            g.memset(mhalf[:], -0.5).then_inc(const_a, 1)
            pool.wait_ge(const_a, 3)
            g.affine_select(out=ident[:], in_=ones[:], compare_op=ALU.is_equal, fill=0.0, base=0,
                            pattern=[[1, P]], channel_multiplier=-1).then_inc(const_a, 1)
            pool.wait_ge(const_a, 4)
            with pool.Fori(0, B) as b:
                for c in range(NCH):
                    n = b * NCH + c
                    for i in range(2):
                        pool.wait_ge(ve_done, 2 * n + i + 1)
                        g.tensor_tensor(rstd[i][:], ve[i][:], mhalf[:], ALU.pow).then_inc(rstd_done, 1)

            phase_a_over(pool)
            g.memset(Ks[0][MROW:MROW + 1, :, :].bitcast(F32), 1.0).then_inc(const_c, 1)
            pool.wait_ge(const_c, 1)
            g.memset(Ks[1][MROW:MROW + 1, :, :].bitcast(F32), 1.0).then_inc(const_c, 1)
            pool.wait_ge(const_c, 2)
            g.iota(later[:], pattern=[[-1, T]], base=T - 1, channel_multiplier=0,
                   allow_small_or_imprecise_dtypes=True).then_inc(const_c, 1)
            pool.wait_ge(const_c, 3)
            g.memset(mx[:], 0.0).then_inc(const_c, 1)
            pool.wait_ge(const_c, 4)
            g.tensor_copy(identb[:], ident[:]).then_inc(const_c, 1)
            pool.wait_ge(const_c, 5)
            g.memset(zrow[:], 0.0).then_inc(const_c, 1)
            pool.wait_ge(const_c, 6)
            g.affine_select(out=zrow[:], in_=zrow[:], compare_op=ALU.is_gt, fill=-BIG, base=P - 1,
                            pattern=[[0, HQ], [0, NT]], channel_multiplier=-1).then_inc(const_c, 1)
            pool.wait_ge(const_c, 7)
            g.memset(zrow[:, :, 0:NT - 1], 0.0).then_inc(const_c, 1)
            pool.wait_ge(const_c, 8)
            g.memset(negm[:], 0.0).then_inc(const_c, 1)
            pool.wait_ge(const_c, 9)
            g.affine_select(out=negm[:], in_=negm[:], compare_op=ALU.is_ge, fill=-BIG, base=0,
                            pattern=[[-1, P]], channel_multiplier=1).then_inc(const_c, 1)
            pool.wait_ge(const_c, 10)

            def quad(qn, par, more, load):
                for s, (c, j) in enumerate(STEPS):
                    r = j - CT * c
                    o = max(0, r) * P
                    step = qn * NSTEP + s
                    A = acc[c % 2]
                    W = A if j == 0 else Pb[ring(s)]
                    if r >= 0:
                        for p in range(NPAIR):
                            pool.wait_ge(exp_done, START + step * NPAIR + p + 1).then_inc(pool_waited, 1)
                            blk = W[p][:, :, o:o + P]
                            g.affine_select(out=blk, in_=blk, compare_op=ALU.is_ge, fill=0.0, base=0,
                                            pattern=[[0, 2], [1, P]], channel_multiplier=-1).then_inc(mask_done, 1)
                    if j % 2:
                        if j == 1:
                            pool.wait_ge(pv_done, START + step)
                        for p in range(NPAIR):
                            if r >= 0:
                                pool.wait_ge(mask_done, qn * NT * NPAIR + (CT * c + r) * NPAIR + p + 1)
                            else:
                                pool.wait_ge(exp_done, START + step * NPAIR + p + 1)
                            pool.wait_ge(sum_done, START + qn * NSUM + sums_before(s) + p - (1 if j > 1 else 0))
                            g.tensor_tensor(A[p][:, :, o:], A[p][:, :, o:], W[p][:, :, o:], ALU.add).then_inc(sum_done, 1)
                    if j == 3:
                        k = qn * NCH + c
                        cols = slice(c * CW, (c + 1) * CW)
                        pool.wait_ge(cum_in[c], (qn + 1) * (32 if c == 0 else 16))
                        g.tensor_tensor(cum[:, cols], tot[:].broadcast_to([P, CW]), cum[:, cols], ALU.subtract).then_inc(sub_done, 1)
                        pool.wait_ge(E_done, START + k + 1)
                        pool.wait_ge(sub_done, START + k + 1)
                        g.tensor_tensor(cum[:, cols], cum[:, cols], E[:, cols], ALU.mult).then_inc(SE_done, 1)
                        pool.wait_ge(SE_done, START + k + 1)
                        g.tensor_tensor(E[:, cols], later[:, cols], E[:, cols], ALU.mult).then_inc(NE_done, 1)

            quads(pool, quad)

        @block.scalar
        def _(act):
            a = nc.scalar
            for k in range(KT):
                act.wait_ge(T_full, k + 1)
                a.copy(wf_t[:, k, :], psT[k % 2][:]).then_inc(wf_done, 1)
            act.wait_ge(bias_in, (2 * KT + 1) * 16)
            with act.Fori(0, B) as b:
                for c in range(NCH):
                    n = b * NCH + c
                    act.wait_ge(P_full, START + n * NPU)
                    for k in range(KT):
                        act.wait_ge(T_full, KT + n * NTU + k + 1)
                        a.copy(xh[:, k, :], psT[k % 2][:]).then_inc(xh_done, 1)
                    for k in range(KT):
                        act.wait_ge(T_full, KT + n * NTU + KT + k + 1)
                        act.wait_ge(yl_done, START + n * KT + max(0, k - 1))
                        a.activation(yf[k % 2][:], psT[k % 2][:], ACT.Identity, bias=bet[:, k:k + 1],
                                     scale=gam[:, k:k + 1]).then_inc(yf_done, 1)
                    for k in range(2 * NQ):
                        act.wait_ge(P_full, START + n * NPU + k + 1)
                        act.wait_ge(st_out[k % 4], START + (n * 2 + k // 4) * 32)
                        a.copy(st_hi[k % 4][:], psP[k % 4][:]).then_inc(hi_done, 1)
                    act.wait_ge(vs_out, START + n * NQ * 16)
                    act.wait_ge(T_full, KT + n * NTU)
                    for j in range(CT):
                        act.wait_ge(P_full, START + n * NPU + 2 * NQ + j + 1)
                        a.copy(vs[:, j, :], psP[j % 4][:]).then_inc(vs_done, 1)
                    for j in range(CT):
                        act.wait_ge(zb_done, START + n * CT + j + 1)
                        act.wait_ge(gs_out[j % 2], START + (n * (CT // 2) + j // 2) * 16)
                        a.activation(gs[j % 2][:], zb[j % 2][:], ACT.Silu).then_inc(gs_done, 1)

            phase_a_over(act)

            def max_rows(m):
                for i in range(2):
                    act.wait_ge(M_full, m * (NMB + 2) + NMB + i + 1)
                    act.wait_ge((mrow_in, m0_out)[i], START + m * 16)
                    a.copy(mrow[i][:], psM[i][0:HQ * NT, 0:P]).then_inc(mrow_done, 1)

            max_rows(0)

            def quad(qn, par, more, load):
                for s, (c, j) in enumerate(STEPS):
                    o = max(0, j - CT * c) * P
                    step = qn * NSTEP + s
                    if j == 0:
                        W = acc[c % 2]
                        act.wait_ge(L_full, START + qn * NCH + c - 1)
                    else:
                        W = Pb[ring(s)]
                        before = ring_before(s)
                        act.wait_ge(pv_done, START + qn * NSTEP + before + 1)
                        if STEPS[before % NSTEP][1] % 2:
                            act.wait_ge(sum_done, START + qn * NSUM + (sums_before(before + 1) if before >= 0 else 0))
                    for p in range(NPAIR):
                        act.wait_ge(S_full, step * NPAIR + p + 1)
                        a.activation(W[p][:, :, o:], psS[p][:, :, o:], ACT.Exp, scale=SCALE).then_inc(exp_done, 1)
                    if j == 2:
                        act.wait_ge(e_in[c], (qn + 1) * HQ * 16)
                        cols = slice(c * CW, (c + 1) * CW)
                        a.activation(E[:, cols], E[:, cols], ACT.Exp, scale=SCALE).then_inc(E_done, 1)
                    if s == MAX_END + 1 and more:
                        max_rows(qn + 1)

            quads(act, quad)

        @block.vector
        def _(dve):
            v = nc.vector
            dve.wait_ge(xt_in[0], 16)
            v.tensor_reduce(wabs[:], xt[0][:], AX.XY, ALU.add, apply_absolute_value=True).then_inc(wabs_done, 1)
            dve.wait_ge(wtot_done, 1)
            v.tensor_scalar(wsc[:, 0:1], psW[:, 0:1], 1.0 / (D * D), EPS, ALU.mult, ALU.add).then_inc(wprep, 1)
            dve.wait_ge(wprep, 1)
            v.tensor_scalar(wsc[:, 1:2], wsc[:, 0:1], 0.5, None, ALU.mult).then_inc(wprep, 1)
            v.tensor_scalar(wsc[:, 2:3], wsc[:, 0:1], -0.5, None, ALU.mult).then_inc(wprep, 1)
            dve.wait_ge(wprep, 3)
            v.tensor_scalar(zn[:], xt[0][:], wsc[:, 2:3], None, ALU.is_lt).then_inc(wprep, 1)
            dve.wait_ge(wprep, 4)
            for k in range(KT):
                v.scalar_tensor_tensor(out=vs[:, k, :], in0=xt[0][:, k, :], scalar=wsc[:, 1:2], in1=zn[:, k, :],
                                       op0=ALU.is_gt, op1=ALU.subtract).then_inc(tern_done, 1)
            dve.wait_ge(tern_done, KT)
            v.tensor_copy(wsc[:, 3:4], wsc[:, 2:3]).then_inc(xt_used, 1)
            for i in range(3):
                st = xt[(i + 1) % 2]
                dve.wait_ge(xt_in[(i + 1) % 2], 16 * ((i + 1) // 2 + 1))
                v.tensor_copy(w_hi[i][:], st[:]).then_inc(wprep, 1)
                dve.wait_ge(wprep, 5 + i)
                v.tensor_tensor(w_lo[i][:], st[:], w_hi[i][:].bitcast(F32), ALU.subtract).then_inc(xt_used, 1)

            def layernorm(n, i, src, dst, done, free):
                own = (2 * n + i) * 2 * CT
                for j in range(CT):
                    v.bn_stats(stats[:, j, :], src[:, j, :]).then_inc(ln_own, 1)
                dve.wait_ge(ln_own, own + CT).then_inc(dve_waited, 1)
                for j in range(CT):
                    v.bn_aggr(mv[i][:, j, :], stats[:, j, :]).then_inc(ln_own, 1)
                dve.wait_ge(ln_own, own + 2 * CT)
                v.tensor_scalar(ve[i][:], mv[i][:, :, 1], EPS, None, ALU.add).then_inc(ve_done, 1)
                dve.wait_ge(rstd_done, 2 * n + i + 1)
                dve.wait_ge(T_full, free)
                for j in range(CT):
                    ins = v.tensor_scalar(dst[:, j, :], src[:, j, :], mv[i][:, j, 0:1], rstd[i][:, j:j + 1],
                                          ALU.subtract, ALU.mult)
                ins.then_inc(done, 1)

            dve.wait_ge(bias_in, (2 * KT + 1) * 16)
            dve.wait_ge(const_a, 4)
            with dve.Fori(0, B) as b:
                for c in range(NCH):
                    n = b * NCH + c
                    dve.wait_ge(xt_in[c % 2], (3 + 2 * b + c // 2) * 16)
                    layernorm(n, 0, xt[c % 2], xn, xt_used, n * NTU if c else KT + n * NTU)
                    dve.wait_ge(xt_used, 4 + n + 1)
                    layernorm(n, 1, xn, zn, zn_done, n * NTU if c else KT + n * NTU)
                    dve.wait_ge(P_full, START + n * NPU)
                    for k in range(KT):
                        dve.wait_ge(xh_done, n * KT + k + 1)
                        v.tensor_tensor(xl[:, k, :], psT[k % 2][:], xh[:, k, :].bitcast(F32), ALU.subtract).then_inc(xl_done, 1)
                    for k in range(KT):
                        dve.wait_ge(yf_done, n * KT + k + 1)
                        v.tensor_copy(yh[:, k, :], yf[k % 2][:]).then_inc(yh_done, 1)
                        dve.wait_ge(yh_done, n * KT + k + 1)
                        v.tensor_tensor(yl[:, k, :], yf[k % 2][:], yh[:, k, :].bitcast(F32), ALU.subtract).then_inc(yl_done, 1)
                    for k in range(2 * NQ):
                        dve.wait_ge(hi_done, n * 2 * NQ + k + 1)
                        v.tensor_tensor(st_lo[k % 4][:], psP[k % 4][:], st_hi[k % 4][:].bitcast(F32), ALU.subtract).then_inc(lo_done, 1)

                    for j in range(CT):
                        dve.wait_ge(P_full, START + n * NPU + 3 * KT + j + 1)
                        dve.wait_ge(gs_done, START + n * CT + max(0, j - 1))
                        v.tensor_tensor(zb[j % 2][:], psP[j % 4][:], bias_b[:], ALU.add).then_inc(zb_done, 1)
                    for m in range(NQ):
                        dve.wait_ge(T_full, KT + n * NTU + 2 * KT + m + 1)
                        dve.wait_ge(cs_out[m], START + n * 16)
                        dve.wait_ge(carry_done, START + n * NQ)
                        v.tensor_tensor_scan(cs[m][:], psT[m % 2][:], zeros[:], 0.0 if c == 0 else carry[:, m:m + 1],
                                             ALU.add, ALU.add).then_inc(cs_done, 1)
                    for m in range(NQ):
                        dve.wait_ge(cs_done, START + n * NQ + m + 1)
                        v.tensor_copy(carry[:, m:m + 1], cs[m][:, CW - 1:CW]).then_inc(carry_done, 1)

            phase_a_over(dve)
            dve.wait_ge(const_c, 10)

            def maxima(m, banks):
                flat = mx[:].rearrange("p a b -> p (a b)")
                for k in banks:
                    _, _, segs, first, step = MAXB[k]
                    w, ns = segs[0][2], len(segs)
                    dve.wait_ge(M_full, m * (NMB + 2) + k + 1)
                    v.tensor_reduce(flat[:, first:first + step * (ns - 1) + 1:step],
                                    psM[k % 2][:, 0:ns * w].rearrange("p (a b) -> p a b", a=ns), AX.X, ALU.max).then_inc(mx_done, 1)

            def row_maxima(m):
                dve.wait_ge(mx_done, START + (m + 1) * NMB)
                v.tensor_reduce(mred[:], mx[:], AX.X, ALU.max).then_inc(mred_done, 1)
                dve.wait_ge(mred_done, 2 * m + 1)
                v.tensor_tensor(mmax[:], mred[:], zrow[:].rearrange("p a b -> p (a b)"), ALU.max).then_inc(mred_done, 1)
                dve.wait_ge(mred_done, 2 * m + 2)
                v.tensor_scalar(mneg[:, 0:HQ * NT], mmax[:], -1.0, None, ALU.mult).then_inc(mneg_done, 1)
                v.tensor_scalar(mneg[:, HQ * NT:], mmax[:], 0.0, -1.0, ALU.max, ALU.mult).then_inc(mneg_done, 1)

            maxima(0, range(NMB))
            row_maxima(0)

            def quad(qn, par, more, load):
                def numerators(c):
                    k = qn * NCH + c
                    dve.wait_ge(pv_done, START + qn * NSTEP + last_step[c] + 1)
                    dve.wait_ge(SE_done, START + k + 1)
                    dve.wait_ge(ost_done, START + k)
                    v.tensor_tensor(num[:], psO[:], cum[:, c * CW:(c + 1) * CW], ALU.add).then_inc(num_done, 1)

                def finish(c, between):
                    k = qn * NCH + c
                    O = ost[c % 2]
                    dve.wait_ge(L_full, START + k + 1)
                    dve.wait_ge(NE_done, START + k + 1)
                    dve.wait_ge(ost_out[c % 2], START + (qn * (NCH // 2) + c // 2) * 16)
                    v.tensor_tensor(O[:], psL[:], E[:, c * CW:(c + 1) * CW], ALU.add).then_inc(add_done, 1)
                    dve.wait_ge(add_done, START + k + 1)
                    for i in range(CT):
                        v.reciprocal(O[:, i * P:(i + 1) * P], O[:, i * P:(i + 1) * P]).then_inc(rec_done, 1)
                        between()
                    dve.wait_ge(rec_done, (k + 1) * CT)
                    dve.wait_ge(num_done, START + k + 1)
                    v.tensor_tensor(O[:], num[:], O[:], ALU.mult).then_inc(ost_done, 1)

                for s, (c, j) in enumerate(STEPS):
                    if j == 0 and c > 0:
                        numerators(c - 1)
                    share = list(max_share(s)) if more else []

                    def some():
                        maxima(qn + 1, share[:1])
                        del share[:1]

                    if j == 1 and c > 0:
                        finish(c - 1, some)
                    maxima(qn + 1, share)
                    if s == MAX_END and more:
                        row_maxima(qn + 1)
                numerators(NCH - 1)
                finish(NCH - 1, lambda: None)

            quads(dve, quad)
            attention_over(dve)
            with dve.Fori(0, B) as b:
                for c in range(NCH):
                    n = b * NCH + c
                    dve.wait_ge(d_in[c % 2], (b * 2 + c // 2 + 1) * 48)
                    dve.wait_ge(oo_out[c % 2], START + (b * 2 + c // 2) * 16)
                    for j in range(CT):
                        dve.wait_ge(D_full, n * CT + j + 1)
                        v.tensor_tensor(sg[j % 2][:], psD[4 * (c % 2) + j][:], gr[c % 2][:, j, :], ALU.mult).then_inc(sg_done, 1)
                        dve.wait_ge(sg_done, START + n * CT + j + 1)
                        v.tensor_tensor(oo[c % 2][:, j, :], sg[j % 2][:], xr[c % 2][:, j, :], ALU.add).then_inc(oo_done, 1)

        @block.tensor
        def _(pe):
            t = nc.tensor
            pe.wait_ge(const_a, 4)
            pe.wait_ge(wabs_done, 1)
            t.matmul(psW[:, 0:1], ones[:], wabs[:], start=True, stop=True).then_inc(wtot_done, 1)
            pe.wait_ge(tern_done, KT)
            for k in range(KT):
                if k >= 2:
                    pe.wait_ge(wf_done, k - 1)
                for i in range(KT):
                    ins = t.transpose(psT[k % 2][:, i * P:(i + 1) * P], vs[:, i, k * P:(k + 1) * P], ident[:])
                ins.then_inc(T_full, 1)
            pe.wait_ge(wf_done, KT)

            with pe.Fori(0, B) as b:
                for c in range(NCH):
                    n = b * NCH + c

                    def transposes(k, src, at):
                        for j in range(CT):
                            ins = t.transpose(psT[k % 2][:, j * P:(j + 1) * P], src[:, j, at * P:(at + 1) * P], ident[:])
                        ins.then_inc(T_full, 1)

                    pe.wait_ge(xt_used, 4 + n + 1)
                    for k in range(KT):
                        if k < 2:
                            pe.wait_ge(cs_done, START + n * NQ)
                        else:
                            pe.wait_ge(xl_done, n * KT + k - 1)
                        transposes(k, xn, k)
                    pe.wait_ge(zn_done, n + 1)
                    for k in range(KT):
                        if k < 2:
                            pe.wait_ge(xl_done, n * KT + KT - 1 + k)
                        else:
                            pe.wait_ge(yf_done, n * KT + k - 1)
                        transposes(k, zn, k)
                    pe.wait_ge(xl_done, (n + 1) * KT)
                    for i in range(2):
                        for m in range(NQ):
                            if i == 0:
                                pe.wait_ge(zb_done, START + n * CT)
                            else:
                                pe.wait_ge(lo_done, n * 2 * NQ + m + 1)
                            cols = slice(m * P, (m + 1) * P)
                            parts = [(w_hi[i], xh), (w_hi[i], xl), (w_lo[i], xh)]
                            for a, (w, xx) in enumerate(parts):
                                for k in range(KT):
                                    ins = t.matmul(psP[m][:], w[:, k, cols], xx[:, k, :], start=(a + k == 0),
                                                   stop=(a == 2 and k == KT - 1))
                            ins.then_inc(P_full, 1)
                    for j in range(CT):
                        pe.wait_ge(lo_done, n * 2 * NQ + NQ + j + 1)
                        cols = slice(j * P, (j + 1) * P)
                        parts = [(xh, w_hi[2]), (xl, w_hi[2]), (xh, w_lo[2])]
                        for a, (xx, w) in enumerate(parts):
                            for k in range(KT):
                                ins = t.matmul(psP[j][:], xx[:, k, cols], w[:, k, :], start=(a + k == 0),
                                               stop=(a == 2 and k == KT - 1))
                        ins.then_inc(P_full, 1)
                    pe.wait_ge(yl_done, START + (n + 1) * KT)
                    for j in range(CT):
                        pe.wait_ge(vs_done, n * CT + j + 1)
                        cols = slice(j * P, (j + 1) * P)
                        for a, yy in enumerate((yh, yl)):
                            for k in range(KT):
                                ins = t.matmul(psP[j][:], yy[:, k, cols], wf_t[:, k, :], start=(a + k == 0),
                                               stop=(a == 1 and k == KT - 1))
                        ins.then_inc(P_full, 1)
                    for m in range(NQ):
                        if m < 2:
                            pe.wait_ge(yf_done, n * KT + KT - 1 + m)
                        else:
                            pe.wait_ge(cs_done, START + n * NQ + m - 1)
                        transposes(m, vs, m)

            phase_a_over(pe)
            pe.wait_ge(const_c, 10)

            def max_scores(m, par, banks):
                Q, K = Qs[par], Ks[par]
                for k in banks:
                    _, h, segs, _, _ = MAXB[k]
                    if k == 0:
                        pe.wait_ge(kq_low[par], (m // 2 + 1) * 96)
                    if k == NLOW:
                        pe.wait_ge(kq_high[par], (m // 2 + 1) * 96)
                    if k < 2:
                        pe.wait_ge(mrow_done, START + 2 * m - 1 + k)
                    else:
                        pe.wait_ge(mx_done, START + m * NMB + k - 1)
                    for z, (tile, k0, w) in enumerate(segs):
                        at = z * w
                        diag = k0 + w == (tile + 1) * P
                        ins = t.matmul(psM[k % 2][:, at:at + w], Q[0:STACK, h, tile * P:(tile + 1) * P],
                                       K[0:STACK, h, k0:k0 + w], start=True, stop=not diag)
                        if diag:
                            ins = t.matmul(psM[k % 2][:, at + w - P:at + w], identb[:], negm[:], start=False, stop=True)
                    ins.then_inc(M_full, 1)

            def max_turn(m):
                for i in range(2):
                    pe.wait_ge(mneg_done, 2 * m + i + 1).then_inc(pe_waited, 1)
                    t.transpose(psM[i][0:HQ * NT, 0:P], mneg[:, i * HQ * NT:(i + 1) * HQ * NT].bitcast(F32), ident[:]).then_inc(M_full, 1)

            max_scores(0, 0, range(NMB))
            max_turn(0)

            def quad(qn, par, more, load):
                Q, K, V = Qs[par], Ks[par], Vs[par]

                def scores(s, p):
                    c, j = STEPS[s]
                    o = max(0, j - CT * c) * P
                    pe.wait_ge(exp_done, START + (qn * NSTEP + s) * NPAIR + p - 1)
                    for e in range(2):
                        h = 2 * p + e
                        ins = t.matmul(psS[p][:, e, o:], K[0:MROW + 1, h, j * P:(j + 1) * P],
                                       Q[0:MROW + 1, h, c * CW + o:(c + 1) * CW], start=True, stop=True)
                    ins.then_inc(S_full, 1)

                def values(s, between):
                    c, j = STEPS[s]
                    r = j - CT * c
                    o = max(0, r) * P
                    step = qn * NSTEP + s
                    W = acc[c % 2] if j == 0 else Pb[ring(s)]
                    if j == 0:
                        pe.wait_ge(num_done, START + qn * NCH + c)
                    own_sum = j % 2 == 0 and j > 0
                    for h in range(HQ):
                        p = h // 2
                        if h % 2 == 0 and r >= 0:
                            pe.wait_ge(mask_done, qn * NT * NPAIR + (CT * c + r) * NPAIR + p + 1)
                        elif h % 2 == 0:
                            pe.wait_ge(exp_done, START + step * NPAIR + p + 1)
                        hc = slice(h * DH, (h + 1) * DH)
                        ins = t.matmul(psO[hc, o:], V[:, j, hc], W[p][:, h % 2, o:],
                                       start=(j == 0), stop=(s == last_step[c]), skip_group_check=True)
                    if own_sum:
                        between()
                        if j == 2:
                            pe.wait_ge(add_done, START + qn * NCH + c)
                        for h in range(HQ):
                            ins = t.matmul(psL[h * DH:(h + 1) * DH, o:], ones[:, 0:DH], W[h // 2][:, h % 2, o:],
                                           start=(j == 2), stop=False, skip_group_check=True)
                    ins.then_inc(pv_done, 1)

                def row_sums(c):
                    pe.wait_ge(sum_done, START + qn * NSUM + sums_before(last_step[c] + 1))
                    for h in range(HQ):
                        ins = t.matmul(psL[h * DH:(h + 1) * DH, :], ones[:, 0:DH], acc[c % 2][h // 2][:, h % 2, :],
                                       start=False, stop=True, skip_group_check=True)
                    ins.then_inc(L_full, 1)

                pe.wait_ge(mrow_in, START + (qn + 1) * 16)
                pe.wait_ge(v_in[par], (qn // 2 + 1) * 16)
                for p in range(NPAIR):
                    scores(0, p)
                for s, (c, j) in enumerate(STEPS):
                    share = list(max_share(s)) if more else []
                    slots = NPAIR + 1 + (1 if j % 2 == 0 and j > 0 else 0)

                    def between():
                        nonlocal slots
                        n = -(-len(share) // slots)
                        slots -= 1
                        max_scores(qn + 1, 1 - par, share[:n])
                        del share[:n]

                    for p in range(NPAIR):
                        if s + 1 < NSTEP:
                            scores(s + 1, p)
                        between()
                    values(s, between)
                    between()
                    if j == 0 and c > 0:
                        row_sums(c - 1)
                    if s == MAX_END + 1 and more:
                        max_turn(qn + 1)
                row_sums(NCH - 1)

            quads(pe, quad)

            attention_over(pe)
            pe.wait_ge(ost_done, START + NQUAD * NCH)
            pe.wait_ge(wo_in, 16)
            with pe.Fori(0, B) as b:
                for c in range(NCH):
                    n = b * NCH + c
                    pe.wait_ge(d_in[c % 2], (b * 2 + c // 2 + 1) * 48)
                    for j in range(CT):
                        pe.wait_ge(sg_done, START + (n * CT if c == 0 else (n - 1) * CT))
                        for k in range(KT):
                            ins = t.matmul(psD[4 * (c % 2) + j][:], ac[c % 2][:, k, j * P:(j + 1) * P], wo[:, k, :],
                                           start=(k == 0), stop=(k == KT - 1))
                        ins.then_inc(D_full, 1)


_INS = ["L0_attn_x", "L0_attn_Wq", "L0_attn_Wk", "L0_attn_Wv", "L0_attn_Wo", "L0_ffn_weight", "L0_ffn_bias",
        "L0_ffn_ln_gamma", "L0_ffn_ln_beta"]


def kernel(**inputs):
    import numpy as np
    import concourse.bacc as bacc
    from concourse.bass_utils import run_bass_kernel_spmd

    nc = bacc.Bacc("TRN2", target_bir_lowering=False, num_devices=1)
    arrays, args = {}, []
    for name in _INS:
        a = np.ascontiguousarray(inputs[name])
        arrays[f"in_{name}"] = a
        args.append(nc.dram_tensor(f"in_{name}", a.shape, mybir.dt.from_np(a.dtype), kind="ExternalInput").ap())
    out = nc.dram_tensor("out_0", (B, T, D), F32, kind="ExternalOutput").ap()
    build(nc, *args, out)
    r = run_bass_kernel_spmd(nc, [arrays], core_ids=[0])
    return r.results[0]["out_0"]
```

```python
from contextlib import ExitStack

import concourse.bass as bass
from concourse import mybir

F32 = mybir.dt.float32
F32R = mybir.dt.float32r
BF16 = mybir.dt.bfloat16
F16 = mybir.dt.float16
ACT = mybir.ActivationFunctionType
ALU = mybir.AluOpType
AX = mybir.AxisListType

P = 128
B, T, D, H = 2, 2048, 512, 16
DH = D // H
KT = D // P
HQ = P // DH
NQ = H // HQ
NQUAD = B * NQ
CW = 512
NCH = T // CW
CT = CW // P
NT = T // P
SCALE = float(T) ** -0.5
EPS = 1e-5
BIG = 1e30
STACK = 3 * DH
MROW = STACK
NSTEP = sum(CT * c + CT for c in range(NCH))
STEPS = [(c, j) for c in range(NCH) for j in range(CT * c + CT)]
NPAIR = HQ // 2
START = 8
MAX_END = NSTEP - CT


def max_banks():
    banks = []
    for i in range(NT):
        for f in range((i + 1) // CT):
            banks.append(([(i, f * CW, CW)], i * CT + f, 1))
    for r in range(1, CT):
        w = r * P
        per = CW // w
        tiles = [i for i in range(NT) if (i + 1) % CT == r]
        for a in range(0, len(tiles), per):
            part = tiles[a:a + per]
            slots = [i * CT + (i + 1) // CT for i in part]
            banks.append(([(i, (i + 1) // CT * CW, w) for i in part], slots[0], CT * CT + 1))
    return banks


MAXB = sorted(((max(i for i, _, _ in segs), h, segs, h * NT * CT + slot, step)
               for h in range(HQ) for segs, slot, step in max_banks()), key=lambda m: m[0] // (NT // 2))
NMB = len(MAXB)
NLOW = sum(m[0] < NT // 2 for m in MAXB)


def width(s):
    c, j = STEPS[s]
    return CW - max(0, j - CT * c) * P


def sums_in_pe(j):
    return j > 0 and j % 2 == 0


def max_slots():
    parts = []
    for s, (c, j) in enumerate(STEPS[:MAX_END]):
        for part in range(HQ + 1 + sums_in_pe(j)):
            parts.append((s, part, width(min(s + 1, NSTEP - 1)) if part < HQ else HQ * width(s)))
    whole, past, k, slots = sum(p[2] for p in parts), 0, 0, {}
    for s, part, time in parts:
        past += time
        upto = NMB * past // whole
        slots[s, part] = range(k, upto)
        k = upto
    return slots


SLOTS = max_slots()


def max_share(s):
    return [k for (step, _), ks in SLOTS.items() if step == s for k in ks]


def ring(s):
    return sum(1 for c, j in STEPS[:s] if j) % 2


def ring_before(s):
    with_ring = [i for i in range(-NSTEP, s) if STEPS[i % NSTEP][1] and ring(i % NSTEP) == ring(s)]
    return with_ring[-1]


def sums_before(s):
    return NPAIR * sum(1 for c, j in STEPS[:s] if j % 2)


NSUM = sums_before(NSTEP)


def build(nc, x, Wq, Wk, Wv, Wo, Wf, bias, gamma, beta, out):
    top = ExitStack()
    with top:
        def sem(name):
            return top.enter_context(nc.semaphore(name))

        def sbuf(stack, name, shape, dt):
            return stack.enter_context(nc.sbuf_tensor(name, shape, dt))

        def psum(stack, name, shape):
            return stack.enter_context(nc.psum_tensor(name, shape, F32))

        q_hi = nc.dram_tensor("q_hi", [B * D, T], F32).ap()
        q_lo = nc.dram_tensor("q_lo", [B * D, T], F32).ap()
        k_hi = nc.dram_tensor("k_hi", [B * D, T], F32).ap()
        k_lo = nc.dram_tensor("k_lo", [B * D, T], F32).ap()
        v_quad = nc.dram_tensor("v_quad", [NQUAD * P, NT * P], F32).ap()
        v_cum = nc.dram_tensor("v_cum", [B * D, T], F32).ap()
        m_rows = nc.dram_tensor("m_rows", [NQUAD * HQ, T], F32).ap()
        gate = nc.dram_tensor("gate", [B * T, D], F32).ap()
        num_t = nc.dram_tensor("num_t", [B * D, T], F32).ap()
        l_rows = nc.dram_tensor("l_rows", [B * H, T], F32).ap()
        r_rows = nc.dram_tensor("r_rows", [B * H, T], F32).ap()

        ident = sbuf(top, "ident", [P, P], F32)
        ones = sbuf(top, "ones", [P, P], F32)

        pa = ExitStack()
        w_hi = [sbuf(pa, f"w_hi{i}", [P, KT, D], F32R) for i in range(3)]
        w_lo = [sbuf(pa, f"w_lo{i}", [P, KT, D], F32R) for i in range(3)]
        wf_t = sbuf(pa, "wf_t", [P, KT, D], F32R)
        xt = [sbuf(pa, f"xt{i}", [P, CT, D], F32) for i in range(2)]
        xn = sbuf(pa, "xn", [P, CT, D], F32)
        zn = sbuf(pa, "zn", [P, CT, D], F32)
        staging = ExitStack()
        w_stage = [sbuf(staging, f"w_stage{i}", [P, KT, D], F32) for i in range(4)]
        staging.close()
        odd = [sbuf(pa, f"{name}1", [P, KT, CW], F32R) for name in ("xh", "xl", "yh", "yl")]
        even = [sbuf(pa, f"{name}0", [P, KT, CW], F32R) for name in ("xh", "xl", "yh", "yl")]
        xh, xl, yh, yl = ([even[i], odd[i]] for i in range(4))
        yf = [sbuf(pa, f"yf{i}", [P, CW], F32) for i in range(2)]
        st_hi = [sbuf(pa, f"st_hi{i}", [P, CW], F32R) for i in range(4)]
        st_lo = [sbuf(pa, f"st_lo{i}", [P, CW], F32R) for i in range(4)]
        vs = sbuf(pa, "vs", [P, CT, D], F32)
        cs = [sbuf(pa, f"cs{i}", [P, CW], F32) for i in range(NQ)]
        carry = sbuf(pa, "carry", [P, NQ], F32)
        zb = [sbuf(pa, f"zb{i}", [P, D], F32) for i in range(2)]
        gs = [sbuf(pa, f"gs{i}", [P, D], F32) for i in range(2)]
        bias_b = sbuf(pa, "bias_b", [P, D], F32)
        zeros = sbuf(pa, "zeros", [P, CW], F32)
        gam = sbuf(pa, "gam", [P, KT], F32)
        bet = sbuf(pa, "bet", [P, KT], F32)
        stats = sbuf(pa, "stats", [P, CT, 6], F32)
        mv = [sbuf(pa, f"mv{i}", [P, CT, 2], F32) for i in range(2)]
        ve = [sbuf(pa, f"ve{i}", [P, CT], F32) for i in range(2)]
        rstd = [sbuf(pa, f"rstd{i}", [P, CT], F32) for i in range(2)]
        mhalf = sbuf(pa, "mhalf", [P, CT], F32)
        wabs = sbuf(pa, "wabs", [P, 1], F32)
        wsc = sbuf(pa, "wsc", [P, 4], F32)
        psT = [psum(pa, f"psT{i}", [P, CW]) for i in range(4)]
        psP = [psum(pa, f"psP{i}", [P, CW]) for i in range(4)]
        psW = psT[3]
        pa.close()

        pc = ExitStack()
        Qs, Ks, Vs = [], [], []
        for i in range(2):
            Qs.append(sbuf(pc, f"Qs{i}", [P, HQ, T], F32R))
            Ks.append(sbuf(pc, f"Ks{i}", [P, HQ, T], F32R))
            Vs.append(sbuf(pc, f"Vs{i}", [P, NT, P], F32))
        Pb = [[sbuf(pc, f"Pb{i}_{p}", [P, 2, CW], F32) for p in range(NPAIR)] for i in range(2)]
        acc = [[sbuf(pc, f"acc{i}_{p}", [P, 2, CW], F32) for p in range(NPAIR)] for i in range(2)]
        cum = sbuf(pc, "cum", [P, T], F32)
        later = sbuf(pc, "later", [P, T], F16)
        E = sbuf(pc, "E", [P, T], F32)
        tot = sbuf(pc, "tot", [P, 1], F32)
        ost = [sbuf(pc, f"ost{i}", [P, CW], F32) for i in range(2)]
        lst = sbuf(pc, "lst", [P, CW], F32)
        identb = sbuf(pc, "identb", [P, P], BF16)
        negm = sbuf(pc, "negm", [P, P], BF16)
        negt = sbuf(pc, "negt", [P, P], BF16)
        zrow = sbuf(pc, "zrow", [P, HQ, NT], F32)
        mx = sbuf(pc, "mx", [P, HQ * NT, CT], F32)
        mred = sbuf(pc, "mred", [P, HQ * NT], F32)
        mmax = sbuf(pc, "mmax", [P, HQ * NT], F32)
        mneg = sbuf(pc, "mneg", [P, 2 * HQ * NT], F32R)
        mrow = [sbuf(pc, f"mrow{i}", [HQ * NT, P], F32R) for i in range(2)]
        psS = [psum(pc, f"psS{i}", [P, 2, CW]) for i in range(2)]
        psM = [psum(pc, f"psM{i}", [P, CW]) for i in range(2)]
        psO = psum(pc, "psO", [P, CW])
        psL = psum(pc, "psL", [P, CW])
        pc.close()

        pd = ExitStack()
        lr = sbuf(pd, "lr", [P, H * T // P], F32)
        wo_h = sbuf(pd, "wo_h", [P, KT, D], F32R)
        wo_l = sbuf(pd, "wo_l", [P, KT, D], F32R)
        ac = [sbuf(pd, f"ac{i}", [P, KT, CW], F32) for i in range(2)]
        rb = [sbuf(pd, f"rb{i}", [P, KT, CW], F32) for i in range(2)]
        ah = [sbuf(pd, "ah0", [P, KT, CW], F32R)]
        al = [sbuf(pd, "al0", [P, KT, CW], F32R)]
        wo_s = rb[1]
        ac += [sbuf(pd, f"ac{i}", [P, KT, CW], F32) for i in range(2, NCH)]
        rb += [sbuf(pd, f"rb{i}", [P, KT, CW], F32) for i in range(2, NCH)]
        ah.append(sbuf(pd, "ah1", [P, KT, CW], F32R))
        al.append(sbuf(pd, "al1", [P, KT, CW], F32R))
        xr = [sbuf(pd, f"xr{i}", [P, CT, D], F32) for i in range(2)]
        gr = [sbuf(pd, f"gr{i}", [P, CT, D], F32) for i in range(2)]
        oo = [sbuf(pd, f"oo{i}", [P, CT, D], F32) for i in range(2)]
        sg = [sbuf(pd, f"sg{i}", [P, D], F32) for i in range(2)]
        psD = [psum(pd, f"psD{i}", [P, D]) for i in range(8)]
        pd.close()

        const_a = sem("const_a")
        bias_in = sem("bias_in")
        xt_in = [sem(f"xt_in{i}") for i in range(2)]
        xt_used = sem("xt_used")
        w_in = [sem(f"w_in{i}") for i in range(4)]
        whi_done = sem("whi_done")
        wlo_done = sem("wlo_done")
        wabs_done = sem("wabs_done")
        wtot_done = sem("wtot_done")
        wprep = sem("wprep")
        tern_done = sem("tern_done")
        wf_done = sem("wf_done")
        T_full = sem("T_full")
        V_full = sem("V_full")
        P_full = sem("P_full")
        ln_own = sem("ln_own")
        dve_waited = sem("dve_waited")
        ve_done = sem("ve_done")
        rstd_done = sem("rstd_done")
        zn_done = sem("zn_done")
        xh_done = sem("xh_done")
        xl_done = sem("xl_done")
        yf_done = sem("yf_done")
        yh_done = sem("yh_done")
        yl_done = sem("yl_done")
        hi_done = sem("hi_done")
        lo_done = sem("lo_done")
        st_out = [sem(f"st_out{i}") for i in range(4)]
        vs_done = sem("vs_done")
        vs_out = sem("vs_out")
        cs_done = sem("cs_done")
        carry_done = sem("carry_done")
        cs_out = [sem(f"cs_out{i}") for i in range(NQ)]
        zb_done = sem("zb_done")
        gs_done = sem("gs_done")
        gs_out = [sem(f"gs_out{i}") for i in range(2)]
        const_c = sem("const_c")
        FOR_MAXIMA, FOR_SCORES = 7, 11
        kq_low = [sem(f"kq_low{i}") for i in range(2)]
        kq_high = [sem(f"kq_high{i}") for i in range(2)]
        v_in = [sem(f"v_in{i}") for i in range(2)]
        cum_in = [sem(f"cum_in{c}") for c in range(NCH)]
        M_full = sem("M_full")
        mx_done = sem("mx_done")
        mred_done = sem("mred_done")
        mneg_done = sem("mneg_done")
        mrow_done = sem("mrow_done")
        mrow_in = sem("mrow_in")
        m0_out = sem("m0_out")
        e_in = [sem(f"e_in{c}") for c in range(NCH)]
        S_full = sem("S_full")
        exp_done = sem("exp_done")
        pool_waited = sem("pool_waited")
        pe_waited = sem("pe_waited")
        sp_waited = sem("sp_waited")
        pv_done = sem("pv_done")
        sum_done = sem("sum_done")
        L_full = sem("L_full")
        E_done = sem("E_done")
        sub_done = sem("sub_done")
        SE_done = sem("SE_done")
        NE_done = sem("NE_done")
        ost_done = sem("ost_done")
        lst_done = sem("lst_done")
        ost_out = [sem(f"ost_out{i}") for i in range(2)]
        lst_out = sem("lst_out")
        wo_in = sem("wo_in")
        wo_done = sem("wo_done")
        lr_in = sem("lr_in")
        lrec_done = sem("lrec_done")
        r_out = sem("r_out")
        r_in = [sem(f"r_in{i}") for i in range(NCH)]
        ac_in = [sem(f"ac_in{i}") for i in range(NCH)]
        xg_in = [sem(f"xg_in{i}") for i in range(2)]
        mul_done = sem("mul_done")
        ah_done = sem("ah_done")
        al_done = sem("al_done")
        D_full = sem("D_full")
        sg_done = sem("sg_done")
        oo_done = sem("oo_done")
        oo_out = [sem(f"oo_out{i}") for i in range(2)]

        x_v = x.rearrange("b (c j p) d -> (b c) p j d", p=P, j=CT)
        out_v = out.rearrange("b (c j p) d -> (b c) p j d", p=P, j=CT)
        gate_t = gate.rearrange("(n p) d -> n p d", p=P)
        gate_v = gate.rearrange("(n j p) d -> n p j d", p=P, j=CT)
        w_q, w_k, w_v, w_o, w_f = (w.rearrange("(k p) n -> p k n", p=P) for w in (Wq, Wk, Wv, Wo, Wf))
        NTU = 2 * KT
        NPU = 3 * KT + CT
        NCHUNK = B * NCH
        last_step = [STEPS.index((c, CT * c + CT - 1)) for c in range(NCH)]

        credited = [P_full, V_full, yf_done, yl_done, zb_done, gs_done, cs_done, carry_done, vs_out,
                    *st_out, *gs_out, *cs_out,
                    mx_done, mrow_done, mrow_in, m0_out, exp_done, pv_done, sum_done, L_full, E_done, sub_done,
                    SE_done, NE_done, ost_done, lst_done, lst_out, *ost_out,
                    mul_done, al_done, D_full, sg_done, oo_done, *oo_out]

        block = top.enter_context(nc.Block())

        def phase_a_over(eng):
            for s in range(4):
                eng.wait_ge(st_out[s], START + NCHUNK * 2 * 32)
            eng.wait_ge(vs_out, START + NCHUNK * NQ * 16)
            for m in range(NQ):
                eng.wait_ge(cs_out[m], START + NCHUNK * 16)
            for s in range(2):
                eng.wait_ge(gs_out[s], START + NCHUNK * (CT // 2) * 16)
            eng.wait_ge(carry_done, START + NCHUNK * NQ)
            eng.wait_ge(T_full, KT + NCHUNK * NTU)
            eng.wait_ge(V_full, START + NCHUNK * NQ)
            eng.wait_ge(P_full, START + NCHUNK * NPU)

        def attention_over(eng):
            for s in range(2):
                eng.wait_ge(ost_out[s], START + NQUAD * NCH // 2 * 16)
            eng.wait_ge(L_full, START + NQUAD * NCH)
            eng.wait_ge(NE_done, START + NQUAD * NCH)
            eng.wait_ge(ost_done, START + NQUAD * NCH)
            eng.wait_ge(lst_out, START + NQUAD * NCH * 16)

        def quads(eng, body):
            with eng.Fori(0, NQUAD // 2 - 1) as i:
                body(2 * i, 0, True, True)
                body(2 * i + 1, 1, True, True)
            body(NQUAD - 2, 0, True, False)
            body(NQUAD - 1, 1, False, False)

        two_banks = [psM[i][:] for i in range(2)]
        six_banks = two_banks + [psS[p][:, e, :] for p in range(NPAIR) for e in range(2)]

        def numerators(b, c):
            return num_t[bass.ds(b * D, D), c * CW:(c + 1) * CW].rearrange("(k p) w -> p k w", p=P)

        def batches(eng, body):
            with eng.Fori(0, B - 1) as b:
                body(b, True)
            body(B - 1, False)

        @block.sync
        def _(sp):
            sp.dma_start(w_stage[0][:], w_f).then_inc(w_in[0], 16)
            sp.dma_start(xt[0][:], x_v[0]).then_inc(xt_in[0], 16)
            sp.dma_start(w_stage[1][:], w_q).then_inc(w_in[1], 16)
            for s in credited:
                sp.sem_inc(s, START)
            for k in range(KT):
                sp.dma_start(gam[:, k:k + 1], gamma.rearrange("(k p u) -> k p u", p=P, u=1)[k]).then_inc(bias_in, 16)
                sp.dma_start(bet[:, k:k + 1], beta.rearrange("(k p u) -> k p u", p=P, u=1)[k]).then_inc(bias_in, 16)
            sp.dma_start(bias_b[:], bias.rearrange("(u n) -> u n", u=1).broadcast_to([P, D])).then_inc(bias_in, 16)
            sp.dma_start(w_stage[2][:], w_k).then_inc(w_in[2], 16)
            sp.dma_start(w_stage[3][:], w_v).then_inc(w_in[3], 16)
            sp.dma_start(xt[1][:], x_v[1]).then_inc(xt_in[1], 16)

            def batch(b, more):
                for c in range(NCH):
                    n = b * NCH + c
                    if more or c < NCH - 2:
                        sp.wait_ge(xt_used, n + 1)
                        sp.dma_start(xt[c % 2][:], x_v[n + 2]).then_inc(xt_in[c % 2], 16)
                    cols = slice(c * CW, (c + 1) * CW)
                    for k in range(2 * NQ):
                        hi, lo = (q_hi, q_lo) if k < NQ else (k_hi, k_lo)
                        rows = bass.ds(b * D + (k % NQ) * P, P)
                        sp.wait_ge(hi_done, n * 2 * NQ + k + 1)
                        sp.dma_start(hi[rows, cols], st_hi[k % 4][:].bitcast(F32)).then_inc(st_out[k % 4], 16)
                        sp.wait_ge(lo_done, n * 2 * NQ + k + 1)
                        sp.dma_start(lo[rows, cols], st_lo[k % 4][:].bitcast(F32)).then_inc(st_out[k % 4], 16)
                    sp.wait_ge(vs_done, (n + 1) * CT)
                    for m in range(NQ):
                        sp.dma_start(v_quad[bass.ds(b * D + m * P, P), cols].rearrange("p (j n) -> p j n", n=P),
                                     vs[:, :, m * P:(m + 1) * P]).then_inc(vs_out, 16)
                    for j in range(CT):
                        sp.wait_ge(gs_done, START + n * CT + j + 1)
                        sp.dma_start(gate_t[n * CT + j], gs[j % 2][:]).then_inc(gs_out[j % 2], 16)
                    for m in range(NQ):
                        sp.wait_ge(cs_done, START + n * NQ + m + 1)
                        sp.dma_start(v_cum[bass.ds(b * D + m * P, P), cols], cs[m][:]).then_inc(cs_out[m], 16)

            batches(sp, batch)

            phase_a_over(sp)

            def load_half(qn, par, half):
                cols = slice(half * T // 2, (half + 1) * T // 2)

                def heads(a):
                    return a[bass.ds(qn * P, P), cols].rearrange("(h d) t -> d h t", d=DH)
                into = (kq_low, kq_high)[half][par]
                for g, (qa, ka) in enumerate(((q_hi, k_hi), (q_lo, k_hi), (q_hi, k_lo))):
                    rows = slice(g * DH, (g + 1) * DH)
                    sp.dma_start(Qs[par][rows, :, cols].bitcast(F32), heads(qa)).then_inc(into, 16)
                    sp.dma_start(Ks[par][rows, :, cols].bitcast(F32), heads(ka)).then_inc(into, 16)

            def load_values(qn, par):
                sp.dma_start(Vs[par][:], v_quad[bass.ds(qn * P, P), :].rearrange("p (j n) -> p j n", n=P)).then_inc(v_in[par], 16)

            def store_maxima(m, par):
                sp.wait_ge(mrow_done, START + 2 * m + 1)
                sp.dma_start(Qs[par][MROW:MROW + 1, :, :].bitcast(F32), mrow[0][:].bitcast(F32)).then_inc(mrow_in, 16)
                sp.wait_ge(mrow_done, START + 2 * m + 2)
                sp.dma_start(m_rows[bass.ds(m * HQ, HQ), :].rearrange("h (i p) -> (h i) p", p=P), mrow[1][:].bitcast(F32)).then_inc(m0_out, 16)

            def chunk_sums(m, c):
                cols = slice(c * CW, (c + 1) * CW)
                sp.wait_ge(SE_done, START + (m - 1) * NCH + c + 1)
                sp.wait_ge(ost_done, START + (m - 1) * NCH + c + 1)
                sp.dma_start(cum[:, cols], v_cum[bass.ds(m * P, P), cols]).then_inc(cum_in[c], 16)
                if c == 0:
                    sp.wait_ge(sub_done, START + m * NCH)
                    sp.dma_start(tot[:], v_cum[bass.ds(m * P, P), T - 1:T],
                                 allow_slow_non_contiguous=True).then_inc(cum_in[c], 16)
                sp.wait_ge(lst_done, START + (m - 1) * NCH + c + 1)
                sp.wait_ge(m0_out, START + (m + 1) * 16)
                for h in range(HQ):
                    sp.dma_start(E[h * DH:(h + 1) * DH, cols],
                                 m_rows[bass.ds(m * HQ + h, 1), cols].broadcast_to([DH, CW])).then_inc(e_in[c], 16)

            def store_chunk(qn, c):
                cols = slice(c * CW, (c + 1) * CW)
                sp.wait_ge(ost_done, START + qn * NCH + c + 1).then_inc(sp_waited, 1)
                sp.dma_start(num_t[bass.ds(qn * P, P), cols], ost[c % 2][:]).then_inc(ost_out[c % 2], 16)
                sp.wait_ge(lst_done, START + qn * NCH + c + 1).then_inc(sp_waited, 1)
                sp.dma_start(l_rows[bass.ds(qn * HQ, HQ), cols], lst[::DH, :]).then_inc(lst_out, 16)

            for half in range(2):
                load_half(0, 0, half)
            load_values(0, 0)
            for half in range(2):
                load_half(1, 1, half)
            load_values(1, 1)
            store_maxima(0, 0)
            for c in range(NCH - 1):
                chunk_sums(0, c)

            def denominators(b):
                sp.dma_start(lr[:], l_rows[bass.ds(b * H, H), :].rearrange("r (a w) -> (r a) w", w=H * T // P)).then_inc(lr_in, 16)

            def reciprocals(b):
                sp.wait_ge(lrec_done, b + 1)
                sp.dma_start(r_rows[bass.ds(b * H, H), :].rearrange("r (a w) -> (r a) w", w=H * T // P), lr[:]).then_inc(r_out, 16)
                sp.wait_ge(r_out, (b + 1) * 16)

            def spread(b, c):
                for k in range(KT):
                    for h in range(HQ):
                        sp.dma_start(rb[c][h * DH:(h + 1) * DH, k, :],
                                     r_rows[bass.ds(b * H + k * HQ + h, 1), c * CW:(c + 1) * CW].broadcast_to([DH, CW])).then_inc(r_in[c], 16)

            def quad(qn, par, more, load):
                chunk_sums(qn, NCH - 1)
                if not more:
                    sp.wait_ge(pv_done, START + (NQUAD - 1) * NSTEP)
                    sp.wait_ge(lst_out, START + NQ * NCH * 16)
                    denominators(0)
                    sp.dma_start(wo_s[:], w_o).then_inc(wo_in, 16)
                store_chunk(qn, 0)
                if not more:
                    reciprocals(0)
                    for i in range(2):
                        sp.wait_ge(ost_out[i], START + NQ * NCH // 2 * 16)
                        sp.dma_start(ac[i][:], numerators(0, i)).then_inc(ac_in[i], 16)
                store_chunk(qn, 1)
                if not more:
                    spread(0, 0)
                store_chunk(qn, 2)
                if not more:
                    sp.wait_ge(wo_done, 2)
                    spread(0, 1)
                if load:
                    sp.wait_ge(pv_done, START + qn * NSTEP + STEPS.index((NCH - 1, NT // 2)))
                    load_half(qn + 2, par, 0)
                if more:
                    store_maxima(qn + 1, 1 - par)
                    for c in range(NCH - 1):
                        chunk_sums(qn + 1, c)
                store_chunk(qn, NCH - 1)
                if load:
                    sp.wait_ge(pv_done, START + (qn + 1) * NSTEP)
                    load_half(qn + 2, par, 1)
                    load_values(qn + 2, par)
            quads(sp, quad)
            attention_over(sp)
            sp.dma_start(ac[2][:], numerators(0, 2)).then_inc(ac_in[2], 16)
            spread(0, 2)

            def batch(b, more):
                if more:
                    denominators(b + 1)
                for c in range(NCH):
                    n = b * NCH + c
                    if c == 0:
                        sp.wait_ge(mul_done, START + n * KT)
                        spread(b, NCH - 1)
                        if more:
                            reciprocals(b + 1)
                    if more and c < NCH - 1:
                        sp.wait_ge(mul_done, START + (n + 1) * KT)
                        spread(b + 1, c)
                    sp.wait_ge(oo_done, START + (n + 1) * CT)
                    sp.dma_start(out_v[n], oo[c % 2][:]).then_inc(oo_out[c % 2], 16)

            batches(sp, batch)
            for s in range(2):
                sp.wait_ge(oo_out[s], START + NCHUNK // 2 * 16)

        @block.gpsimd
        def _(pool):
            g = nc.gpsimd
            g.memset(ones[:], 1.0).then_inc(const_a, 1)
            g.memset(zeros[:], 0.0).then_inc(const_a, 1)
            g.memset(mhalf[:], -0.5).then_inc(const_a, 1)
            pool.wait_ge(const_a, 3)
            g.affine_select(out=ident[:], in_=ones[:], compare_op=ALU.is_equal, fill=0.0, base=0,
                            pattern=[[1, P]], channel_multiplier=-1).then_inc(const_a, 1)
            pool.wait_ge(const_a, 4)
            with pool.Fori(0, B) as b:
                for c in range(NCH):
                    n = b * NCH + c
                    for i in range(2):
                        pool.wait_ge(ve_done, 2 * n + i + 1)
                        g.tensor_tensor(rstd[i][:], ve[i][:], mhalf[:], ALU.pow).then_inc(rstd_done, 1)

            phase_a_over(pool)
            g.memset(mx[:], 0.0).then_inc(const_c, 1)
            pool.wait_ge(const_c, 1)
            g.tensor_copy(identb[:], ident[:]).then_inc(const_c, 1)
            pool.wait_ge(const_c, 2)
            g.memset(negm[:], 0.0).then_inc(const_c, 1)
            pool.wait_ge(const_c, 3)
            g.affine_select(out=negm[:], in_=negm[:], compare_op=ALU.is_ge, fill=-BIG, base=0,
                            pattern=[[-1, P]], channel_multiplier=1).then_inc(const_c, 1)
            pool.wait_ge(const_c, 4)
            g.memset(zrow[:], 0.0).then_inc(const_c, 1)
            pool.wait_ge(const_c, 5)
            g.affine_select(out=zrow[:], in_=zrow[:], compare_op=ALU.is_gt, fill=-BIG, base=P - 1,
                            pattern=[[0, HQ], [0, NT]], channel_multiplier=-1).then_inc(const_c, 1)
            pool.wait_ge(const_c, 6)
            g.memset(zrow[:, :, 0:NT - 1], 0.0).then_inc(const_c, 1)
            pool.wait_ge(const_c, FOR_MAXIMA)
            g.memset(negt[:], 0.0).then_inc(const_c, 1)
            pool.wait_ge(const_c, 8)
            g.affine_select(out=negt[:], in_=negt[:], compare_op=ALU.is_ge, fill=-BIG, base=0,
                            pattern=[[1, P]], channel_multiplier=-1).then_inc(const_c, 1)
            pool.wait_ge(const_c, 9)
            g.memset(Ks[0][MROW:MROW + 1, :, :].bitcast(F32), 1.0).then_inc(const_c, 1)
            pool.wait_ge(const_c, 10)
            g.memset(Ks[1][MROW:MROW + 1, :, :].bitcast(F32), 1.0).then_inc(const_c, 1)
            pool.wait_ge(const_c, FOR_SCORES)
            g.iota(later[:], pattern=[[-1, T]], base=T - 1, channel_multiplier=0,
                   allow_small_or_imprecise_dtypes=True).then_inc(const_c, 1)
            pool.wait_ge(const_c, 12)

            def quad(qn, par, more, load):
                for s, (c, j) in enumerate(STEPS):
                    o = max(0, j - CT * c) * P
                    step = qn * NSTEP + s
                    if j == (1 if c == 0 else 3):
                        k = qn * NCH + c
                        cols = slice(c * CW, (c + 1) * CW)
                        pool.wait_ge(sub_done, START + k + 1)
                        pool.wait_ge(E_done, START + k + 1)
                        g.tensor_tensor(cum[:, cols], cum[:, cols], E[:, cols], ALU.mult).then_inc(SE_done, 1)
                        pool.wait_ge(SE_done, START + k + 1)
                        g.tensor_tensor(E[:, cols], later[:, cols], E[:, cols], ALU.mult).then_inc(NE_done, 1)
                    if j % 2:
                        if j == 1:
                            pool.wait_ge(pv_done, START + step)
                        for p in range(NPAIR):
                            pool.wait_ge(exp_done, START + step * NPAIR + p + 1)
                            pool.wait_ge(sum_done, START + qn * NSUM + sums_before(s) + p - (1 if j > 1 else 0))
                            g.tensor_tensor(acc[c % 2][p][:, :, o:], acc[c % 2][p][:, :, o:], Pb[ring(s)][p][:, :, o:], ALU.add).then_inc(sum_done, 1)

            quads(pool, quad)

            with pool.Fori(0, B) as b:
                for c in range(NCH):
                    pool.wait_ge(ac_in[c], (b + 1) * 16)
                    pool.wait_ge(r_in[c], (b + 1) * H * 16)
                    for k in range(KT):
                        g.tensor_tensor(ac[c][:, k, :], ac[c][:, k, :], rb[c][:, k, :], ALU.mult).then_inc(mul_done, 1)

        @block.scalar
        def _(act):
            a = nc.scalar

            def weight_high(i):
                act.wait_ge(w_in[i + 1], 16)
                a.copy(w_hi[i][:], w_stage[i + 1][:]).then_inc(whi_done, 1)

            weight_high(0)
            for k in range(KT):
                act.wait_ge(T_full, k + 1)
                a.copy(wf_t[:, k, :], psT[k % 2][:]).then_inc(wf_done, 1)

            def x_high(m, l, k):
                act.wait_ge(T_full, KT + m * NTU + k + 1)
                a.copy(xh[l % 2][:, k, :], psT[k % 2][:]).then_inc(xh_done, 1)

            def y_whole(m, k):
                act.wait_ge(T_full, KT + m * NTU + KT + k + 1)
                act.wait_ge(yl_done, START + m * KT + max(0, k - 1))
                a.activation(yf[k % 2][:], psT[k % 2][:], ACT.Identity, bias=bet[:, k:k + 1],
                             scale=gam[:, k:k + 1]).then_inc(yf_done, 1)

            for k in range(KT):
                x_high(0, 0, k)
            act.wait_ge(bias_in, (2 * KT + 1) * 16)
            for k in range(KT):
                y_whole(0, k)
            weight_high(1)
            weight_high(2)

            def batch(b, more):
                for c in range(NCH):
                    n = b * NCH + c
                    ahead = more or c < NCH - 1
                    act.wait_ge(P_full, START + n * NPU)
                    for k in range(2 * NQ):
                        act.wait_ge(P_full, START + n * NPU + k + 1)
                        act.wait_ge(st_out[k % 4], START + (n * 2 + k // 4) * 32)
                        a.copy(st_hi[k % 4][:], psP[k % 4][:]).then_inc(hi_done, 1)
                        if k >= NQ and ahead:
                            x_high(n + 1, c + 1, k - NQ)
                    act.wait_ge(vs_out, START + n * NQ * 16)
                    act.wait_ge(V_full, START + n * NQ)
                    for j in range(CT):
                        act.wait_ge(P_full, START + n * NPU + 2 * NQ + j + 1)
                        a.copy(vs[:, j, :], psP[j % 4][:]).then_inc(vs_done, 1)
                        if ahead:
                            y_whole(n + 1, j)
                    for j in range(CT):
                        act.wait_ge(zb_done, START + n * CT + j + 1)
                        act.wait_ge(gs_out[j % 2], START + (n * (CT // 2) + j // 2) * 16)
                        a.activation(gs[j % 2][:], zb[j % 2][:], ACT.Silu).then_inc(gs_done, 1)

            batches(act, batch)

            phase_a_over(act)

            def max_rows(m):
                for i in range(2):
                    act.wait_ge(M_full, m * (NMB + 2) + NMB + i + 1)
                    act.wait_ge((mrow_in, m0_out)[i], START + m * 16)
                    a.copy(mrow[i][:], psM[i][0:HQ * NT, 0:P]).then_inc(mrow_done, 1)

            max_rows(0)

            def quad(qn, par, more, load):
                for s, (c, j) in enumerate(STEPS):
                    o = max(0, j - CT * c) * P
                    step = qn * NSTEP + s
                    if j == 0:
                        W = acc[c % 2]
                        act.wait_ge(L_full, START + qn * NCH + c - 1)
                    else:
                        W = Pb[ring(s)]
                        before = ring_before(s)
                        act.wait_ge(pv_done, START + qn * NSTEP + before + 1)
                        if STEPS[before % NSTEP][1] % 2:
                            act.wait_ge(sum_done, START + qn * NSUM + (sums_before(before + 1) if before >= 0 else 0))
                    for p in range(NPAIR):
                        act.wait_ge(S_full, step * NPAIR + p + 1)
                        a.activation(W[p][:, :, o:], psS[p][:, :, o:], ACT.Exp, scale=SCALE).then_inc(exp_done, 1)
                    if j == (0 if c == 0 else 2):
                        act.wait_ge(e_in[c], (qn + 1) * HQ * 16)
                        cols = slice(c * CW, (c + 1) * CW)
                        a.activation(E[:, cols], E[:, cols], ACT.Exp, scale=SCALE).then_inc(E_done, 1)
                        act.wait_ge(cum_in[c], (qn + 1) * (32 if c == 0 else 16))
                        a.activation(cum[:, cols], cum[:, cols], ACT.Identity, bias=tot[:, 0:1], scale=-1.0).then_inc(sub_done, 1)
                    if s == MAX_END + 1 and more:
                        max_rows(qn + 1)

            quads(act, quad)

            def high(n, c):
                act.wait_ge(D_full, START + (n - 1) * CT)
                for k in range(KT):
                    act.wait_ge(mul_done, START + n * KT + k + 1)
                    a.copy(ah[c % 2][:, k, :], ac[c][:, k, :]).then_inc(ah_done, 1)

            def load_xg(n, c):
                act.dma_start(xr[c % 2][:], x_v[n]).then_inc(xg_in[c % 2], 16)
                act.dma_start(gr[c % 2][:], gate_v[n]).then_inc(xg_in[c % 2], 16)

            high(0, 0)
            attention_over(act)
            load_xg(0, 0)

            def batch(b, more):
                for c in range(NCH):
                    n = b * NCH + c
                    follows = more or c < NCH - 1
                    if follows:
                        high(n + 1, (c + 1) % NCH)
                    if c == 0:
                        act.wait_ge(al_done, START + n * KT)
                        act.dma_start(ac[NCH - 1][:], numerators(b, NCH - 1)).then_inc(ac_in[NCH - 1], 16)
                    if more and c < NCH - 1:
                        act.wait_ge(al_done, START + (n + 1) * KT)
                        act.dma_start(ac[c][:], numerators(b + 1, c)).then_inc(ac_in[c], 16)
                    if follows:
                        act.wait_ge(oo_done, START + n * CT)
                        load_xg(n + 1, (c + 1) % NCH)

            batches(act, batch)

        @block.vector
        def _(dve):
            v = nc.vector
            dve.wait_ge(w_in[0], 16)
            v.tensor_reduce(wabs[:], w_stage[0][:], AX.XY, ALU.add, apply_absolute_value=True).then_inc(wabs_done, 1)
            dve.wait_ge(wtot_done, 1)
            v.tensor_scalar(wsc[:, 0:1], psW[:, 0:1], 1.0 / (D * D), EPS, ALU.mult, ALU.add).then_inc(wprep, 1)
            dve.wait_ge(wprep, 1)
            v.tensor_scalar(wsc[:, 1:2], wsc[:, 0:1], 0.5, None, ALU.mult).then_inc(wprep, 1)
            v.tensor_scalar(wsc[:, 2:3], wsc[:, 0:1], -0.5, None, ALU.mult).then_inc(wprep, 1)
            dve.wait_ge(wprep, 3)
            v.tensor_scalar(zn[:], w_stage[0][:], wsc[:, 2:3], None, ALU.is_lt).then_inc(wprep, 1)
            dve.wait_ge(wprep, 4)
            for k in range(KT):
                v.scalar_tensor_tensor(out=vs[:, k, :], in0=w_stage[0][:, k, :], scalar=wsc[:, 1:2], in1=zn[:, k, :],
                                       op0=ALU.is_gt, op1=ALU.subtract).then_inc(tern_done, 1)
            dve.wait_ge(tern_done, KT)

            def weight_low(i):
                dve.wait_ge(whi_done, i + 1)
                v.tensor_tensor(w_lo[i][:], w_stage[i + 1][:], w_hi[i][:].bitcast(F32), ALU.subtract).then_inc(wlo_done, 1)

            def layernorm(n, i, src, dst, done, free):
                own = (2 * n + i) * 2 * CT
                for j in range(CT):
                    v.bn_stats(stats[:, j, :], src[:, j, :]).then_inc(ln_own, 1)
                dve.wait_ge(ln_own, own + CT).then_inc(dve_waited, 1)
                for j in range(CT):
                    v.bn_aggr(mv[i][:, j, :], stats[:, j, :]).then_inc(ln_own, 1)
                dve.wait_ge(ln_own, own + 2 * CT)
                v.tensor_scalar(ve[i][:], mv[i][:, :, 1], EPS, None, ALU.add).then_inc(ve_done, 1)
                dve.wait_ge(rstd_done, 2 * n + i + 1)
                dve.wait_ge(T_full, free)
                for j in range(CT):
                    ins = v.tensor_scalar(dst[:, j, :], src[:, j, :], mv[i][:, j, 0:1], rstd[i][:, j:j + 1],
                                          ALU.subtract, ALU.mult)
                ins.then_inc(done, 1)

            dve.wait_ge(const_a, 4)
            def norm(b, l, i):
                m = b * NCH + l
                if i == 0:
                    dve.wait_ge(xt_in[l % 2], (2 * b + l // 2 + 1) * 16)
                    layernorm(m, 0, xt[l % 2], xn, xt_used, KT + m * NTU)
                else:
                    dve.wait_ge(xt_used, m + 1)
                    layernorm(m, 1, xn, zn, zn_done, KT + m * NTU)

            def x_low(m, l, k):
                dve.wait_ge(xh_done, m * KT + k + 1)
                v.tensor_tensor(xl[l % 2][:, k, :], psT[k % 2][:], xh[l % 2][:, k, :].bitcast(F32), ALU.subtract).then_inc(xl_done, 1)

            def y_parts(m, l, k):
                dve.wait_ge(yf_done, START + m * KT + k + 1)
                v.tensor_copy(yh[l % 2][:, k, :], yf[k % 2][:]).then_inc(yh_done, 1)
                dve.wait_ge(yh_done, m * KT + k + 1)
                v.tensor_tensor(yl[l % 2][:, k, :], yf[k % 2][:], yh[l % 2][:, k, :].bitcast(F32), ALU.subtract).then_inc(yl_done, 1)

            norm(0, 0, 0)
            norm(0, 0, 1)
            for k in range(KT):
                x_low(0, 0, k)
            weight_low(0)
            for k in range(KT):
                y_parts(0, 0, k)
            weight_low(1)
            weight_low(2)
            dve.wait_ge(bias_in, (2 * KT + 1) * 16)

            def batch(b, more):
                for c in range(NCH):
                    n = b * NCH + c

                    def low(k):
                        dve.wait_ge(hi_done, n * 2 * NQ + k + 1)
                        v.tensor_tensor(st_lo[k % 4][:], psP[k % 4][:], st_hi[k % 4][:].bitcast(F32), ALU.subtract).then_inc(lo_done, 1)

                    ahead = more or c < NCH - 1
                    if ahead:
                        norm(b, c + 1, 0)
                    low(0)
                    low(1)
                    if ahead:
                        norm(b, c + 1, 1)
                    low(2)
                    low(3)
                    for k in range(KT):
                        low(NQ + k)
                        if ahead:
                            x_low(n + 1, c + 1, k)
                    if ahead:
                        for k in range(KT):
                            y_parts(n + 1, c + 1, k)
                    for j in range(CT):
                        dve.wait_ge(P_full, START + n * NPU + 3 * KT + j + 1)
                        dve.wait_ge(gs_done, START + n * CT + max(0, j - 1))
                        v.tensor_tensor(zb[j % 2][:], psP[j % 4][:], bias_b[:], ALU.add).then_inc(zb_done, 1)
                    for m in range(NQ):
                        dve.wait_ge(V_full, START + n * NQ + m + 1)
                        dve.wait_ge(cs_out[m], START + n * 16)
                        dve.wait_ge(carry_done, START + n * NQ)
                        v.tensor_tensor_scan(cs[m][:], psT[2 + m % 2][:], zeros[:], 0.0 if c == 0 else carry[:, m:m + 1],
                                             ALU.add, ALU.add).then_inc(cs_done, 1)
                    for m in range(NQ):
                        dve.wait_ge(cs_done, START + n * NQ + m + 1)
                        v.tensor_copy(carry[:, m:m + 1], cs[m][:, CW - 1:CW]).then_inc(carry_done, 1)

            batches(dve, batch)

            phase_a_over(dve)
            dve.wait_ge(const_c, FOR_MAXIMA)

            def maxima(m, ks, banks=two_banks):
                flat = mx[:].rearrange("p a b -> p (a b)")
                for k in ks:
                    _, _, segs, first, step = MAXB[k]
                    w, ns = segs[0][2], len(segs)
                    dve.wait_ge(M_full, m * (NMB + 2) + k + 1)
                    v.tensor_reduce(flat[:, first:first + step * (ns - 1) + 1:step],
                                    banks[k % len(banks)][:, 0:ns * w].rearrange("p (a b) -> p a b", a=ns), AX.X, ALU.max).then_inc(mx_done, 1)

            def row_maxima(m):
                dve.wait_ge(mx_done, START + (m + 1) * NMB)
                v.tensor_reduce(mred[:], mx[:], AX.X, ALU.max).then_inc(mred_done, 1)
                dve.wait_ge(mred_done, 2 * m + 1)
                v.tensor_tensor(mmax[:], mred[:], zrow[:].rearrange("p a b -> p (a b)"), ALU.max).then_inc(mred_done, 1)
                dve.wait_ge(mred_done, 2 * m + 2)
                v.tensor_scalar(mneg[:, 0:HQ * NT], mmax[:], -1.0, None, ALU.mult).then_inc(mneg_done, 1)
                v.tensor_scalar(mneg[:, HQ * NT:], mmax[:], 0.0, -1.0, ALU.max, ALU.mult).then_inc(mneg_done, 1)

            def reciprocals(b):
                dve.wait_ge(lr_in, (b + 1) * 16)
                v.reciprocal(lr[:], lr[:]).then_inc(lrec_done, 1)

            maxima(0, range(NMB), six_banks)
            row_maxima(0)

            def quad(qn, par, more, load):
                def numerators(c):
                    k = qn * NCH + c
                    dve.wait_ge(pv_done, START + qn * NSTEP + last_step[c] + 1)
                    dve.wait_ge(SE_done, START + k + 1)
                    dve.wait_ge(ost_out[c % 2], START + (qn * (NCH // 2) + c // 2) * 16)
                    v.tensor_tensor(ost[c % 2][:], psO[:], cum[:, c * CW:(c + 1) * CW], ALU.add).then_inc(ost_done, 1)

                def denominators(c):
                    k = qn * NCH + c
                    dve.wait_ge(L_full, START + k + 1)
                    dve.wait_ge(NE_done, START + k + 1)
                    dve.wait_ge(lst_out, START + k * 16)
                    v.tensor_tensor(lst[:], psL[:], E[:, c * CW:(c + 1) * CW], ALU.add).then_inc(lst_done, 1)

                for s, (c, j) in enumerate(STEPS):
                    if j == 0 and c > 0:
                        numerators(c - 1)
                    if j == 1 and c > 0:
                        denominators(c - 1)
                        if c == 1 and not more:
                            reciprocals(0)
                            dve.wait_ge(wo_in, 16)
                            v.tensor_copy(wo_h[:], wo_s[:]).then_inc(wo_done, 1)
                            dve.wait_ge(wo_done, 1)
                            v.tensor_tensor(wo_l[:], wo_s[:], wo_h[:].bitcast(F32), ALU.subtract).then_inc(wo_done, 1)
                    if more:
                        maxima(qn + 1, max_share(s))
                    if s == MAX_END and more:
                        row_maxima(qn + 1)
                numerators(NCH - 1)
                denominators(NCH - 1)

            quads(dve, quad)

            def low(n, c):
                for k in range(KT):
                    dve.wait_ge(ah_done, n * KT + k + 1)
                    v.tensor_tensor(al[c % 2][:, k, :], ac[c][:, k, :], ah[c % 2][:, k, :].bitcast(F32), ALU.subtract).then_inc(al_done, 1)

            low(0, 0)

            def batch(b, more):
                for c in range(NCH):
                    n = b * NCH + c
                    if more or c < NCH - 1:
                        low(n + 1, (c + 1) % NCH)
                    if more and c == 0:
                        reciprocals(b + 1)
                    dve.wait_ge(xg_in[c % 2], (b * 2 + c // 2 + 1) * 32)
                    dve.wait_ge(oo_out[c % 2], START + (b * 2 + c // 2) * 16)
                    for j in range(CT):
                        dve.wait_ge(D_full, START + n * CT + j + 1)
                        v.tensor_tensor(sg[j % 2][:], psD[4 * (c % 2) + j][:], gr[c % 2][:, j, :], ALU.mult).then_inc(sg_done, 1)
                        dve.wait_ge(sg_done, START + n * CT + j + 1)
                        v.tensor_tensor(oo[c % 2][:, j, :], sg[j % 2][:], xr[c % 2][:, j, :], ALU.add).then_inc(oo_done, 1)

            batches(dve, batch)

        @block.tensor
        def _(pe):
            t = nc.tensor
            pe.wait_ge(const_a, 4)
            pe.wait_ge(wabs_done, 1)
            t.matmul(psW[:, 0:1], ones[:], wabs[:], start=True, stop=True).then_inc(wtot_done, 1)
            pe.wait_ge(tern_done, KT)
            for k in range(KT):
                if k >= 2:
                    pe.wait_ge(wf_done, k - 1)
                for i in range(KT):
                    ins = t.transpose(psT[k % 2][:, i * P:(i + 1) * P], vs[:, i, k * P:(k + 1) * P], ident[:])
                ins.then_inc(T_full, 1)
            pe.wait_ge(wf_done, KT)

            def transposes(bank, src, at, full):
                for j in range(CT):
                    ins = t.transpose(psT[bank][:, j * P:(j + 1) * P], src[:, j, at * P:(at + 1) * P], ident[:])
                ins.then_inc(full, 1)

            def turn_x(m, k):
                pe.wait_ge(xt_used, m + 1)
                if k < 2:
                    pe.wait_ge(yf_done, START + m * KT + k - 1)
                else:
                    pe.wait_ge(xl_done, m * KT + k - 1)
                transposes(k % 2, xn, k, T_full)

            def turn_z(m, k):
                pe.wait_ge(zn_done, m + 1)
                if k < 2:
                    pe.wait_ge(xl_done, m * KT + KT - 1 + k)
                else:
                    pe.wait_ge(yf_done, START + m * KT + k - 1)
                transposes(k % 2, zn, k, T_full)

            for k in range(KT):
                turn_x(0, k)
            for k in range(KT):
                turn_z(0, k)

            def batch(b, more):
                for c in range(NCH):
                    n = b * NCH + c
                    X, XL, Y, YL = xh[c % 2], xl[c % 2], yh[c % 2], yl[c % 2]
                    ahead = more or c < NCH - 1
                    pe.wait_ge(xl_done, (n + 1) * KT)
                    for i in range(2):
                        for m in range(NQ):
                            if i == 0:
                                pe.wait_ge(zb_done, START + (n - 1) * CT + m + 1)
                            else:
                                pe.wait_ge(lo_done, n * 2 * NQ + m + 1)
                            cols = slice(m * P, (m + 1) * P)
                            parts = [(w_hi[i], X), (w_hi[i], XL), (w_lo[i], X)]
                            for a, (w, xx) in enumerate(parts):
                                if a != 1:
                                    pe.wait_ge((whi_done, None, wlo_done)[a], i + 1)
                                for k in range(KT):
                                    ins = t.matmul(psP[m][:], w[:, k, cols], xx[:, k, :], start=(a + k == 0),
                                                   stop=(a == 2 and k == KT - 1))
                            ins.then_inc(P_full, 1)
                            if i and ahead:
                                turn_x(n + 1, m)
                    for j in range(CT):
                        pe.wait_ge(lo_done, n * 2 * NQ + NQ + j + 1)
                        cols = slice(j * P, (j + 1) * P)
                        parts = [(X, w_hi[2]), (XL, w_hi[2]), (X, w_lo[2])]
                        for a, (xx, w) in enumerate(parts):
                            if a != 1:
                                pe.wait_ge((whi_done, None, wlo_done)[a], 3)
                            for k in range(KT):
                                ins = t.matmul(psP[j][:], xx[:, k, cols], w[:, k, :], start=(a + k == 0),
                                               stop=(a == 2 and k == KT - 1))
                        ins.then_inc(P_full, 1)
                        if ahead:
                            turn_z(n + 1, j)
                    pe.wait_ge(yl_done, START + (n + 1) * KT)
                    for j in range(CT):
                        pe.wait_ge(vs_done, n * CT + j + 1)
                        cols = slice(j * P, (j + 1) * P)
                        for a, yy in enumerate((Y, YL)):
                            for k in range(KT):
                                ins = t.matmul(psP[j][:], yy[:, k, cols], wf_t[:, k, :], start=(a + k == 0),
                                               stop=(a == 1 and k == KT - 1))
                        ins.then_inc(P_full, 1)
                    for m in range(NQ):
                        pe.wait_ge(cs_done, START + n * NQ + m - 1)
                        transposes(2 + m % 2, vs, m, V_full)

            batches(pe, batch)

            phase_a_over(pe)
            pe.wait_ge(const_c, FOR_MAXIMA)

            def max_scores(m, par, ks, banks=two_banks):
                Q, K = Qs[par], Ks[par]
                for k in ks:
                    _, h, segs, _, _ = MAXB[k]
                    if k == 0:
                        pe.wait_ge(kq_low[par], (m // 2 + 1) * 96)
                    if k == NLOW:
                        pe.wait_ge(kq_high[par], (m // 2 + 1) * 96)
                    if k < 2:
                        pe.wait_ge(mrow_done, START + 2 * m - 1 + k)
                    elif k >= len(banks):
                        pe.wait_ge(mx_done, START + m * NMB + k - len(banks) + 1)
                    bank = banks[k % len(banks)]
                    for z, (tile, k0, w) in enumerate(segs):
                        at = z * w
                        diag = k0 + w == (tile + 1) * P
                        ins = t.matmul(bank[:, at:at + w], Q[0:STACK, h, tile * P:(tile + 1) * P],
                                       K[0:STACK, h, k0:k0 + w], start=True, stop=not diag)
                        if diag:
                            ins = t.matmul(bank[:, at + w - P:at + w], identb[:], negm[:], start=False, stop=True)
                    ins.then_inc(M_full, 1)

            def max_turn(m):
                for i in range(2):
                    pe.wait_ge(mneg_done, 2 * m + i + 1).then_inc(pe_waited, 1)
                    t.transpose(psM[i][0:HQ * NT, 0:P], mneg[:, i * HQ * NT:(i + 1) * HQ * NT].bitcast(F32), ident[:]).then_inc(M_full, 1)

            max_scores(0, 0, range(NMB), six_banks)
            max_turn(0)
            pe.wait_ge(const_c, FOR_SCORES)

            def quad(qn, par, more, load):
                Q, K, V = Qs[par], Ks[par], Vs[par]

                def scores(s, p, between=None):
                    c, j = STEPS[s]
                    o = max(0, j - CT * c) * P
                    pe.wait_ge(exp_done, START + (qn * NSTEP + s) * NPAIR + p - 1)
                    for e in range(2):
                        h = 2 * p + e
                        ins = t.matmul(psS[p][:, e, o:], K[0:MROW + 1, h, j * P:(j + 1) * P],
                                       Q[0:MROW + 1, h, c * CW + o:(c + 1) * CW], start=True, stop=j < CT * c)
                        if j >= CT * c:
                            ins = t.matmul(psS[p][:, e, o:o + P], identb[:], negt[:], start=False, stop=True)
                        if e:
                            ins.then_inc(S_full, 1)
                        if between:
                            between(h)

                def values(s, between):
                    c, j = STEPS[s]
                    r = j - CT * c
                    o = max(0, r) * P
                    step = qn * NSTEP + s
                    W = acc[c % 2] if j == 0 else Pb[ring(s)]
                    if j == 0:
                        pe.wait_ge(ost_done, START + qn * NCH + c)
                    for h in range(HQ):
                        p = h // 2
                        if h % 2 == 0:
                            pe.wait_ge(exp_done, START + step * NPAIR + p + 1)
                        hc = slice(h * DH, (h + 1) * DH)
                        ins = t.matmul(psO[hc, o:], V[:, j, hc], W[p][:, h % 2, o:],
                                       start=(j == 0), stop=(s == last_step[c]), skip_group_check=True)
                    if sums_in_pe(j):
                        between(HQ)
                        if j == 2:
                            pe.wait_ge(lst_done, START + qn * NCH + c)
                        for h in range(HQ):
                            ins = t.matmul(psL[h * DH:(h + 1) * DH, o:], ones[:, 0:DH], W[h // 2][:, h % 2, o:],
                                           start=(j == 2), stop=False, skip_group_check=True)
                    ins.then_inc(pv_done, 1)

                def row_sums(c):
                    pe.wait_ge(sum_done, START + qn * NSUM + sums_before(last_step[c] + 1))
                    for h in range(HQ):
                        ins = t.matmul(psL[h * DH:(h + 1) * DH, :], ones[:, 0:DH], acc[c % 2][h // 2][:, h % 2, :],
                                       start=False, stop=True, skip_group_check=True)
                    ins.then_inc(L_full, 1)

                pe.wait_ge(mrow_in, START + (qn + 1) * 16)
                pe.wait_ge(v_in[par], (qn // 2 + 1) * 16)
                for p in range(NPAIR):
                    scores(0, p)
                for s, (c, j) in enumerate(STEPS):
                    def between(part):
                        if more:
                            max_scores(qn + 1, 1 - par, SLOTS.get((s, part), ()))

                    for p in range(NPAIR):
                        if s + 1 < NSTEP:
                            scores(s + 1, p, between)
                    values(s, between)
                    between(HQ + sums_in_pe(j))
                    if j == 0 and c > 0:
                        row_sums(c - 1)
                    if s == MAX_END + 1 and more:
                        max_turn(qn + 1)
                row_sums(NCH - 1)

            quads(pe, quad)

            pe.wait_ge(ost_done, START + NQUAD * NCH)
            pe.wait_ge(lst_done, START + NQUAD * NCH)
            pe.wait_ge(wo_done, 2)
            with pe.Fori(0, B) as b:
                for c in range(NCH):
                    n = b * NCH + c
                    A, L, out_banks = ah[c % 2], al[c % 2], psD[4 * (c % 2):4 * (c % 2) + 4]
                    for j in range(CT):
                        pe.wait_ge(sg_done, START + (n - 2) * CT + j + 1)
                        for k in range(KT):
                            if j == 0:
                                pe.wait_ge(ah_done, n * KT + k + 1)
                            for w in (wo_h, wo_l):
                                t.matmul(out_banks[j][:], A[:, k, j * P:(j + 1) * P], w[:, k, :],
                                         start=(k == 0 and w is wo_h), stop=False)
                    pe.wait_ge(al_done, START + (n + 1) * KT)
                    for j in range(CT):
                        for k in range(KT):
                            ins = t.matmul(out_banks[j][:], L[:, k, j * P:(j + 1) * P], wo_h[:, k, :],
                                           start=False, stop=(k == KT - 1))
                        ins.then_inc(D_full, 1)


_INS = ["L0_attn_x", "L0_attn_Wq", "L0_attn_Wk", "L0_attn_Wv", "L0_attn_Wo", "L0_ffn_weight", "L0_ffn_bias",
        "L0_ffn_ln_gamma", "L0_ffn_ln_beta"]


def kernel(**inputs):
    import numpy as np
    import concourse.bacc as bacc
    from concourse.bass_utils import run_bass_kernel_spmd

    nc = bacc.Bacc("TRN2", target_bir_lowering=False, num_devices=1)
    arrays, args = {}, []
    for name in _INS:
        a = np.ascontiguousarray(inputs[name])
        arrays[f"in_{name}"] = a
        args.append(nc.dram_tensor(f"in_{name}", a.shape, mybir.dt.from_np(a.dtype), kind="ExternalInput").ap())
    out = nc.dram_tensor("out_0", (B, T, D), F32, kind="ExternalOutput").ap()
    build(nc, *args, out)
    r = run_bass_kernel_spmd(nc, [arrays], core_ids=[0])
    return r.results[0]["out_0"]
```
